# Optimizing a Trainium2 kernel written in Bass

```python
import numpy as np
import jax
import jax.numpy as jnp

def _softmax(x, axis=-1):
    return jax.nn.softmax(x, axis=axis)

def _gelu(x):
    return jax.nn.gelu(x, approximate=True)

def _silu(x):
    return jax.nn.silu(x)

def _sigmoid(x):
    return jax.nn.sigmoid(x)

def _layernorm(x, axis=-1, eps=1e-05):
    m = jnp.mean(x, axis=axis, keepdims=True)
    v = jnp.var(x, axis=axis, keepdims=True)
    return (x - m) / jnp.sqrt(v + eps)

def _scatter_add(tgt, idx, src, axis=0):
    return tgt.at[idx].add(src)

def _segment_sum(src, seg, n):
    return jax.ops.segment_sum(src, seg, n)
kernel_name = 'mk_recurrent_d1_jaxref_r8_6585af'

def setup_inputs(seed: int=0):
    np.random.seed(seed)
    _w = jnp.asarray

    def _L0_attn_setup():
        import jax, jax.numpy as jnp
        import numpy as np
        B, N, D_MODEL, H, D_HEAD = (1, 256, 128, 16, 64)
        A0, A1, LIM = (1.0, 1.0, 1.0)

        def _fastmax_causal_p1(q, k, v):
            qn = jnp.max(jnp.linalg.norm(q, axis=-1), axis=-1)[..., None, None]
            kn = jnp.max(jnp.linalg.norm(k, axis=-1), axis=-1)[..., None, None]
            q = LIM * q / qn
            k = LIM * k / kn
            n = q.shape[2]
            kv = jnp.cumsum(k[..., :, None] * v[..., None, :], axis=2)
            num = A0 * jnp.cumsum(v, axis=2) + A1 * jnp.einsum('bhnd,bhnde->bhne', q, kv)
            ksum = jnp.cumsum(k, axis=2)
            den = A0 * jnp.arange(1, n + 1, dtype=q.dtype) + A1 * jnp.einsum('bhnd,bhnd->bhn', q, ksum)
            return num / den[..., None]
        key = jax.random.key(seed)
        ks = jax.random.split(key, 6)
        s = 1.0 / np.sqrt(D_MODEL).astype(np.float32)
        return {'X': jax.random.normal(ks[0], (B, N, D_MODEL), jnp.float32), 'Wq': jax.random.normal(ks[1], (H * D_HEAD, D_MODEL), jnp.float32) * s, 'Wk': jax.random.normal(ks[2], (H * D_HEAD, D_MODEL), jnp.float32) * s, 'Wv': jax.random.normal(ks[3], (H * D_HEAD, D_MODEL), jnp.float32) * s, 'Wo': jax.random.normal(ks[4], (D_MODEL, H * D_HEAD), jnp.float32) * s, 'bo': jnp.zeros((D_MODEL,), jnp.float32)}
    _L0_attn_in = _L0_attn_setup()

    def _L0_ffn_setup():
        import jax, jax.numpy as jnp
        import numpy as np
        DIM = 128
        HIDDEN = 384
        SCALE = 1.0 / 127.0

        def _dequant(w_int, dtype):
            return w_int.astype(dtype) * jnp.asarray(SCALE, dtype)
        key = jax.random.key(seed)
        k_x, k_g, k_u, k_d = jax.random.split(key, 4)
        x = jax.random.normal(k_x, (4, 256, DIM), dtype=jnp.float32)
        w_gate = jax.random.randint(k_g, (HIDDEN, DIM), -127, 128, dtype=jnp.int32)
        w_up = jax.random.randint(k_u, (HIDDEN, DIM), -127, 128, dtype=jnp.int32)
        w_down = jax.random.randint(k_d, (DIM, HIDDEN), -127, 128, dtype=jnp.int32)
        return {'x': x, 'w_gate': w_gate, 'w_up': w_up, 'w_down': w_down}
    _L0_ffn_in = _L0_ffn_setup()
    _d = {'L0_attn_X': _L0_attn_in['X'], 'L0_attn_Wq': _L0_attn_in['Wq'], 'L0_attn_Wk': _L0_attn_in['Wk'], 'L0_attn_Wv': _L0_attn_in['Wv'], 'L0_attn_Wo': _L0_attn_in['Wo'], 'L0_attn_bo': _L0_attn_in['bo'], 'L0_ffn_w_gate': _L0_ffn_in['w_gate'], 'L0_ffn_w_up': _L0_ffn_in['w_up'], 'L0_ffn_w_down': _L0_ffn_in['w_down']}
    _x0 = _d['L0_attn_X']
    _d['L0_attn_X'] = jax.random.normal(jax.random.fold_in(jax.random.key(seed), 1), (16, 512, 128), dtype=_x0.dtype)
    del _x0
    return _d

def reference(L0_attn_X, L0_attn_Wq, L0_attn_Wk, L0_attn_Wv, L0_attn_Wo, L0_attn_bo, L0_ffn_w_gate, L0_ffn_w_up, L0_ffn_w_down):

    def _L0_attn_ref(X, Wq, Wk, Wv, Wo, bo):
        import jax, jax.numpy as jnp
        import numpy as np
        B, N, D_MODEL, H, D_HEAD = (1, 256, 128, 16, 64)
        A0, A1, LIM = (1.0, 1.0, 1.0)

        def _fastmax_causal_p1(q, k, v):
            qn = jnp.max(jnp.linalg.norm(q, axis=-1), axis=-1)[..., None, None]
            kn = jnp.max(jnp.linalg.norm(k, axis=-1), axis=-1)[..., None, None]
            q = LIM * q / qn
            k = LIM * k / kn
            n = q.shape[2]
            kv = jnp.cumsum(k[..., :, None] * v[..., None, :], axis=2)
            num = A0 * jnp.cumsum(v, axis=2) + A1 * jnp.einsum('bhnd,bhnde->bhne', q, kv)
            ksum = jnp.cumsum(k, axis=2)
            den = A0 * jnp.arange(1, n + 1, dtype=q.dtype) + A1 * jnp.einsum('bhnd,bhnd->bhn', q, ksum)
            return num / den[..., None]
        b, n, _ = X.shape

        def heads(W):
            return (X @ W.T).reshape(b, n, H, D_HEAD).transpose(0, 2, 1, 3)
        q, k, v = (heads(Wq), heads(Wk), heads(Wv))
        vh = _fastmax_causal_p1(q, k, v)
        vh = vh.transpose(0, 2, 1, 3).reshape(b, n, H * D_HEAD)
        return vh @ Wo.T + bo

    def _L0_ffn_ref(x, w_gate, w_up, w_down):
        import jax, jax.numpy as jnp
        import numpy as np
        DIM = 128
        HIDDEN = 384
        SCALE = 1.0 / 127.0

        def _dequant(w_int, dtype):
            return w_int.astype(dtype) * jnp.asarray(SCALE, dtype)
        wg = _dequant(w_gate, x.dtype)
        wu = _dequant(w_up, x.dtype)
        wd = _dequant(w_down, x.dtype)
        gate = jnp.einsum('bsd,hd->bsh', x, wg)
        up = jnp.einsum('bsd,hd->bsh', x, wu)
        h = jax.nn.silu(gate) * up
        return jnp.einsum('bsh,dh->bsd', h, wd)
    x = L0_attn_X
    xn = _layernorm(x, axis=-1)
    s = _L0_attn_ref(xn, L0_attn_Wq, L0_attn_Wk, L0_attn_Wv, L0_attn_Wo, L0_attn_bo)
    g = _silu(_L0_ffn_ref(xn, L0_ffn_w_gate, L0_ffn_w_up, L0_ffn_w_down))
    x = x + s * g
    return x

_drawn_inputs = setup_inputs


def setup_inputs(seed=0):
    import zlib

    import numpy as np

    out = dict(_drawn_inputs(seed))
    spreads = {'L0_attn_bo': (0.0, 0.1)}
    factors = {}
    for name, (base, spread) in spreads.items():
        noise = np.random.default_rng([zlib.crc32(name.encode()), seed]).standard_normal(out[name].shape)
        drawn = base * np.exp(spread * noise) if base else spread * noise
        out[name] = jnp.asarray(drawn.astype(out[name].dtype))
    for name, factor in factors.items():
        out[name] = (out[name] * factor).astype(out[name].dtype)
    return out
```

```python
from contextlib import ExitStack

import concourse.bass as bass
from concourse import mybir

ALU = mybir.AluOpType
ACT = mybir.ActivationFunctionType
AX = mybir.AxisListType
F32 = mybir.dt.float32
I32 = mybir.dt.int32

P = 128
DH = 64
VE = DH + 1
LN_EPS = 1e-5
DEQUANT = 1.0 / 127.0


def build(nc, X, WqT, WkT, WvT, WoT, bo, WgT, WuT, WdT, out):
    NB, N, D = X.shape
    HD = WqT.shape[1]
    FF = WgT.shape[1]
    C = N // P
    NP = HD // P
    NF = FF // P
    assert D == P and N == C * P and C == 4 and NP == 8 and NF == 3

    x_dram = X.rearrange("b (c p) d -> b p c d", p=P)
    out_dram = out.rearrange("b (c p) d -> b p c d", p=P)

    with ExitStack() as ctx:
        def sb(name, shape, dt=F32):
            return ctx.enter_context(nc.sbuf_tensor(name, shape, dt))

        def pb(name):
            return ctx.enter_context(nc.psum_tensor(name, [P, 512], F32))

        def sem(name):
            return ctx.enter_context(nc.semaphore(name))

        wq = sb("wq", [P, HD])
        wk = sb("wk", [P, HD])
        wv = sb("wv", [P, HD])
        wo = sb("wo", [P, NP, D])
        bo_col = sb("bo_col", [P, 1])
        wg_i = sb("wg_i", [P, FF], I32)
        wu_i = sb("wu_i", [P, FF], I32)
        wd_i = sb("wd_i", [P, NF, D], I32)
        wg = sb("wg", [P, FF])
        wu = sb("wu", [P, FF])
        wd = sb("wd", [P, NF, D])
        ident = sb("ident", [P, P])
        ones = sb("ones", [P, P])
        causal = sb("causal", [P, C, P])
        head_sum = sb("head_sum", [P, 32])
        norm_pick = sb("norm_pick", [64, 4])
        half = sb("half", [P, 4])
        minus_half = sb("minus_half", [P, C])
        x_in = sb("x_in", [P, C, D])
        x_res = sb("x_res", [P, C, D])
        ln_stats = sb("ln_stats", [P, C, 6])
        ln_sum = sb("ln_sum", [P, C])
        ln_gap = sb("ln_gap", [P, C])
        ln_dev = sb("ln_dev", [P, C])
        ln_gap2 = sb("ln_gap2", [P, C])
        ln_dev2 = sb("ln_dev2", [P, C])
        ln_mean = sb("ln_mean", [P, C])
        ln_var = sb("ln_var", [P, C])
        ln_rstd = sb("ln_rstd", [P, C])
        xn = sb("xn", [P, C, D])
        xnT = sb("xnT", [P, N])
        silu_gate = sb("silu_gate", [P, N])
        hidden = sb("hidden", [P, NF, N])
        gate = sb("gate", [P, N])
        mixed = sb("mixed", [P, N])
        out_sb = sb("out_sb", [P, C, D])
        qT = sb("qT", [P, 2, N])
        kT = sb("kT", [P, 2, N])
        v1 = sb("v1", [P, 2, C, 2, VE])
        v_sum = sb("v_sum", [P, 2, 2, VE])
        v_past = sb("v_past", [P, 3, 2, VE])
        q_sq = sb("q_sq", [P, N])
        k_sq = sb("k_sq", [P, N])
        k_tok = sb("k_tok", [P, 3, P])
        state = sb("state", [P, 3, 2, VE])
        weights = sb("weights", [P, 2, C, P])
        norm_max = sb("norm_max", [64, 1])
        norm_cols = sb("norm_cols", [64, 4])
        norm_sq = sb("norm_sq", [P, 4])
        norm = sb("norm", [P, 4])
        a = sb("a", [P, 2])
        rden = sb("rden", [P, C, 2, 1])
        o = sb("o", [P, C, 2, DH])
        oT = sb("oT", [P, N])

        b_s = [pb("b_s0"), pb("b_s1")]
        b_q = pb("b_q")
        b_k = pb("b_k")
        b_v = pb("b_v")
        b_oT = pb("b_oT")
        b_x = pb("b_x")
        b_y = pb("b_y")

        def o_bank(i):
            return b_s[i][:, 0:4 * VE].rearrange("p (c h e) -> p c h e", c=2, h=2)

        st_ps = b_v[:, 0:3 * VE].rearrange("p (c e) -> p c e", c=3)
        nb_ps = b_v[:, 256:260]

        weights_in = sem("weights_in")
        x_loaded = sem("x_loaded")
        out_stored = sem("out_stored")
        ffn_w_ready = sem("ffn_w_ready")
        pool_const = sem("pool_const")
        zero_fill = sem("zero_fill")
        stats_done = sem("stats_done")
        moment_step = sem("moment_step")
        mean_ready = sem("mean_ready")
        var_ready = sem("var_ready")
        rstd_ready = sem("rstd_ready")
        xn_ready = sem("xn_ready")
        xnT_ps = sem("xnT_ps")
        xnT_ready = sem("xnT_ready")
        x_res_ready = sem("x_res_ready")
        q_ps = sem("q_ps")
        q_ready = sem("q_ready")
        q_sq_ready = sem("q_sq_ready")
        k_ps = sem("k_ps")
        k_ready = sem("k_ready")
        k_sq_ready = sem("k_sq_ready")
        v_ps = sem("v_ps")
        v_ready = sem("v_ready")
        v_sum_a = sem("v_sum_a")
        v_sum_ready = sem("v_sum_ready")
        v_past_ready = sem("v_past_ready")
        norms_ps = sem("norms_ps")
        norm_max_ready = sem("norm_max_ready")
        norm_cols_ready = sem("norm_cols_ready")
        nb_ready = sem("nb_ready")
        norm_sq_ready = sem("norm_sq_ready")
        norm_ready = sem("norm_ready")
        a_ready = sem("a_ready")
        k_tok_ps = sem("k_tok_ps")
        k_tok_ready = sem("k_tok_ready")
        state_ps = sem("state_ps")
        state_part = sem("state_part")
        scores_ps = sem("scores_ps")
        weights_ready = sem("weights_ready")
        o_ps = sem("o_ps")
        rden_ready = sem("rden_ready")
        o_ready = sem("o_ready")
        oT_ps = sem("oT_ps")
        oT_ready = sem("oT_ready")
        y_part = sem("y_part")
        mixed_ready = sem("mixed_ready")
        gate_h_ps = sem("gate_h_ps")
        silu_h_ready = sem("silu_h_ready")
        up_ps = sem("up_ps")
        hidden_ready = sem("hidden_ready")
        ffn_ps = sem("ffn_ps")
        gate_ready = sem("gate_ready")
        final_ps = sem("final_ps")
        out_ready = sem("out_ready")

        def some(count):
            return not isinstance(count, int) or count > 0

        def batches(eng, body):
            body(0, True, False)
            with eng.Fori(1, NB - 1) as b:
                body(b, False, False)
            body(NB - 1, False, True)

        block = ctx.enter_context(nc.Block())

        @block.sync
        def _(sp):
            def load_x(b):
                sp.dma_start(x_in[:, :, :], x_dram[b]).then_inc(x_loaded, 16)

            def store(b):
                sp.wait_ge(out_ready, b + 1)
                sp.dma_start(out_dram[b], out_sb[:, :, :]).then_inc(out_stored, 16)

            load_x(0)
            for dst, src in ((wq[:, :], WqT), (wk[:, :], WkT), (wv[:, :], WvT),
                             (wg_i[:, :], WgT), (wu_i[:, :], WuT)):
                sp.dma_start(dst, src).then_inc(weights_in, 16)
            sp.dma_start(wd_i[:, :, :], WdT.rearrange("(t p) d -> p t d", p=P)).then_inc(weights_in, 16)
            sp.dma_start(wo[:, :, :], WoT.rearrange("(t p) d -> p t d", p=P)).then_inc(weights_in, 16)
            sp.dma_start(bo_col[:, :], bo.rearrange("(p o) -> p o", o=1)).then_inc(weights_in, 16)

            def body(b, first, last):
                if not first:
                    store(b - 1)
                if not last:
                    sp.wait_ge(x_res_ready, b + 1)
                    sp.wait_ge(xn_ready, b + 1)
                    load_x(b + 1)

            batches(sp, body)
            store(NB - 1)
            sp.wait_ge(out_stored, 16 * NB)

        @block.gpsimd
        def _(pool):
            pool.memset(ident[:, :], 0.0).then_inc(zero_fill, 1)
            pool.memset(causal[:, :, :], 1.0).then_inc(zero_fill, 1)
            pool.memset(head_sum[:, :], 0.0).then_inc(zero_fill, 1)
            pool.memset(norm_pick[:, :], 0.0).then_inc(zero_fill, 1)
            pool.memset(ones[:, :], 1.0).then_inc(pool_const, 1)
            pool.memset(half[:, :], 0.5).then_inc(pool_const, 1)
            pool.memset(minus_half[:, :], -0.5).then_inc(pool_const, 1)
            pool.memset(state[:, :, :, :], 0.0).then_inc(pool_const, 1)
            pool.memset(v1[:, :, :, :, :], 1.0).then_inc(pool_const, 1)
            pool.wait_ge(zero_fill, 4)
            pool.affine_select(out=ident[:, :], in_=ident[:, :], compare_op=ALU.not_equal, fill=1.0, base=0,
                               pattern=[[-1, P]], channel_multiplier=1).then_inc(pool_const, 1)
            pool.affine_select(out=causal[:, :, :], in_=causal[:, :, :], compare_op=ALU.is_ge, fill=0.0, base=0,
                               pattern=[[0, C], [1, P]], channel_multiplier=-1).then_inc(pool_const, 1)
            for h in range(2):
                pool.wait_ge(pool_const, 7 + h)
                pool.memset(head_sum[h * DH:(h + 1) * DH, h:h + 1], 1.0).then_inc(pool_const, 1)
            for g in range(2):
                pool.wait_ge(pool_const, 9 + g)
                pool.affine_select(out=norm_pick[32 * g:32 * g + 32, 2 * g:2 * g + 2],
                                   in_=norm_pick[32 * g:32 * g + 32, 2 * g:2 * g + 2],
                                   compare_op=ALU.not_equal, fill=1.0, base=0,
                                   pattern=[[-1, 2]], channel_multiplier=1).then_inc(pool_const, 1)

            def ln_rstd_of(b):
                pool.wait_ge(var_ready, b + 1)
                pool.tensor_tensor(ln_rstd[:, :], ln_var[:, :], minus_half[:, :], ALU.pow).then_inc(rstd_ready, 1)

            def value_sums(n, par):
                pool.wait_ge(v_ready, n + 1)
                if some(n):
                    pool.wait_ge(v_past_ready, n)
                pool.tensor_tensor(v_sum[:, 0], v1[:, par, 0], v1[:, par, 1], ALU.add).then_inc(v_sum_a, 1)
                pool.wait_ge(v_sum_a, n + 1)
                pool.tensor_tensor(v_sum[:, 1], v_sum[:, 0], v1[:, par, 2], ALU.add).then_inc(v_sum_ready, 1)

            def head_scale(n):
                pool.wait_ge(norm_sq_ready, n + 1)
                pool.tensor_tensor(norm[:, :], norm_sq[:, :], half[:, :], ALU.pow).then_inc(norm_ready, 1)
                pool.wait_ge(norm_ready, n + 1)
                if some(2 * n):
                    pool.wait_ge(weights_ready, 2 * n)
                if some(n):
                    pool.wait_ge(v_past_ready, n)
                pool.tensor_tensor(a[:, :], norm[:, 0:2], norm[:, 2:4], ALU.mult).then_inc(a_ready, 1)

            def project_part(n, par):
                value_sums(n, par)
                head_scale(n)

            pool.wait_ge(pool_const, 11)
            ln_rstd_of(0)
            project_part(0, 0)

            def body(b, first, last):
                for t in range(NP):
                    u = b * NP + t
                    if t == 5 and not last:
                        ln_rstd_of(b + 1)
                    if not (last and t == NP - 1):
                        project_part(u + 1, (t + 1) % 2)

            batches(pool, body)

        @block.tensor
        def _(pe):
            def project_qk(n, t, par):
                if some(n):
                    pe.wait_ge(norm_max_ready, n)
                pe.matmul(b_q[:, :], wq[:, t * P:(t + 1) * P], xnT[:, :], start=True, stop=True)\
                    .then_inc(q_ps, 1)
                if some(n):
                    pe.wait_ge(k_tok_ready, n)
                pe.matmul(b_k[:, :], wk[:, t * P:(t + 1) * P], xnT[:, :], start=True, stop=True)\
                    .then_inc(k_ps, 1)

            def project_v(n, t):
                if some(6 * n):
                    pe.wait_ge(state_part, 6 * n)
                if some(n):
                    pe.wait_ge(norm_sq_ready, n)
                for c in range(C):
                    mm = pe.matmul(b_v[:, c * P:(c + 1) * P], xnT[:, c * P:(c + 1) * P], wv[:, t * P:(t + 1) * P],
                                   start=True, stop=True)
                mm.then_inc(v_ps, 1)

            def norms(n):
                pe.wait_ge(q_ready, n + 1)
                pe.wait_ge(q_sq_ready, n + 1)
                pe.matmul(b_q[0:32, :], head_sum[:, :], q_sq[:, :], start=True, stop=True)
                pe.wait_ge(k_sq_ready, n + 1)
                pe.matmul(b_q[32:64, :], head_sum[:, :], k_sq[:, :], start=True, stop=True)\
                    .then_inc(norms_ps, 1)

            def keys_by_token(n, par):
                pe.wait_ge(k_ready, n + 1)
                for c in range(3):
                    mm = pe.transpose(b_k[:, c * P:(c + 1) * P], kT[:, par, c * P:(c + 1) * P], ident[:, :])
                mm.then_inc(k_tok_ps, 1)

            def states(n, par):
                pe.wait_ge(k_tok_ready, n + 1)
                pe.wait_ge(v_ready, n + 1)
                for c in range(3):
                    for h in range(2):
                        mm = pe.matmul(st_ps[h * DH:(h + 1) * DH, c], k_tok[:, c, h * DH:(h + 1) * DH],
                                       v1[:, par, c, h, :], start=True, stop=True)
                mm.then_inc(state_ps, 1)

            def spread_norms(n):
                pe.wait_ge(norm_cols_ready, n + 1)
                pe.matmul(nb_ps, ones[0:64, :], norm_cols[:, :], start=True, stop=True).then_inc(nb_ready, 1)

            def scores(u, par):
                pe.wait_ge(q_ready, u + 1)
                pe.wait_ge(k_ready, u + 1)
                if some(2 * u):
                    pe.wait_ge(o_ready, 2 * u)
                for h in range(2):
                    for c in range(C):
                        rows = slice(h * DH, (h + 1) * DH)
                        mm = pe.matmul(b_s[h][:, c * P:(c + 1) * P], kT[rows, par, c * P:(c + 1) * P],
                                       qT[rows, par, c * P:(c + 1) * P], start=True, stop=True)
                    mm.then_inc(scores_ps, 1)

            def attend(u, par):
                pe.wait_ge(v_past_ready, u + 1)
                pe.wait_ge(weights_ready, 2 * u + 2)
                pe.wait_ge(state_part, 6 * (u + 1))
                for i in range(2):
                    ob = o_bank(i)
                    c0 = 1 if i == 0 else 2
                    c1 = 2 if i == 0 else 4
                    pe.matmul(ob[:, c0 - 2 * i:c1 - 2 * i], ones[:, :], v_past[:, c0 - 1:c1 - 1],
                              start=True, stop=False, skip_group_check=True)
                    for c in range(2 * i, 2 * i + 2):
                        if c > 0:
                            pe.matmul(ob[:, c - 2 * i], qT[:, par, c * P:(c + 1) * P], state[:, c - 1],
                                      start=False, stop=False, skip_group_check=True)
                        for h in range(2):
                            mm = pe.matmul(ob[:, c - 2 * i, h], weights[:, h, c], v1[:, par, c, h, :],
                                           start=False, stop=True, skip_group_check=True)
                    mm.then_inc(o_ps, 1)

            def turn_outputs(u):
                pe.wait_ge(o_ready, 2 * (u + 1))
                if some(u):
                    pe.wait_ge(oT_ready, u)
                for c in range(C):
                    mm = pe.transpose(b_oT[:, c * P:(c + 1) * P], o[:, c].rearrange("p h e -> p (h e)"), ident[:, :])
                mm.then_inc(oT_ps, 1)

            def project_out(u, t, mixed_before):
                pe.wait_ge(oT_ready, u + 1)
                if t == 0:
                    if some(mixed_before):
                        pe.wait_ge(mixed_ready, mixed_before)
                pe.matmul(b_y[:, :], wo[:, t, :], oT[:, :], start=(t == 0), stop=(t == NP - 1),
                          skip_group_check=True).then_inc(y_part, 1)

            def ffn_gate(b, f):
                if f == 0:
                    pe.wait_ge(xnT_ready, b + 1)
                else:
                    pe.wait_ge(hidden_ready, b * NF + f)
                if f == 2:
                    if some(b):
                        pe.wait_ge(out_ready, b)
                pe.matmul(b_x[:, :], wg[:, f * P:(f + 1) * P], xnT[:, :], start=True, stop=True)\
                    .then_inc(gate_h_ps, 1)

            def ffn_up(b, f):
                pe.wait_ge(silu_h_ready, b * NF + f + 1)
                pe.matmul(b_x[:, :], wu[:, f * P:(f + 1) * P], xnT[:, :], start=True, stop=True)\
                    .then_inc(up_ps, 1)

            def ffn_down(b):
                pe.wait_ge(hidden_ready, (b + 1) * NF)
                for f in range(NF):
                    mm = pe.matmul(b_x[:, :], wd[:, f, :], hidden[:, f, :], start=(f == 0), stop=(f == NF - 1))
                mm.then_inc(ffn_ps, 1)

            def turn_xn(b):
                pe.wait_ge(xn_ready, b + 1)
                if some(b):
                    pe.wait_ge(gate_ready, b)
                for c in range(C):
                    mm = pe.transpose(b_x[:, c * P:(c + 1) * P], xn[:, c, :], ident[:, :])
                mm.then_inc(xnT_ps, 1)

            def turn_mixed(b, hidden_count):
                pe.wait_ge(mixed_ready, b + 1)
                pe.wait_ge(hidden_ready, hidden_count)
                for c in range(C):
                    mm = pe.transpose(b_x[:, c * P:(c + 1) * P], mixed[:, c * P:(c + 1) * P], ident[:, :])
                mm.then_inc(final_ps, 1)

            pe.wait_ge(pool_const, 11)
            turn_xn(0)
            pe.wait_ge(weights_in, 16 * 8)
            pe.wait_ge(ffn_w_ready, 3)
            pe.wait_ge(xnT_ready, 1)
            project_qk(0, 0, 0)
            project_v(0, 0)
            norms(0)
            keys_by_token(0, 0)
            states(0, 0)
            spread_norms(0)

            def body(b, first, last):
                for t in range(NP):
                    u = b * NP + t
                    par = t % 2
                    nt, npar = (t + 1) % NP, (t + 1) % 2
                    more = not (last and t == NP - 1)
                    scores(u, par)
                    if not (first and t == 0):
                        project_out(u - 1, (t - 1) % NP, b)
                    if t < 2:
                        ffn_gate(b, t)
                    if t == 2 and not first:
                        turn_mixed(b - 1, b * NF + 2)
                    if t == 3:
                        ffn_down(b)
                    if more:
                        if t == NP - 1:
                            pe.wait_ge(xnT_ready, b + 2)
                        project_qk(u + 1, nt, npar)
                        project_v(u + 1, nt)
                    if t == 2:
                        ffn_gate(b, 2)
                    attend(u, par)
                    if more:
                        norms(u + 1)
                        keys_by_token(u + 1, npar)
                    if t < NF:
                        ffn_up(b, t)
                    if t == 6 and not last:
                        turn_xn(b + 1)
                    turn_outputs(u)
                    if more:
                        states(u + 1, npar)
                        spread_norms(u + 1)

            batches(pe, body)
            project_out(NB * NP - 1, NP - 1, NB - 1)
            pe.wait_ge(gate_ready, NB)
            turn_mixed(NB - 1, NB * NF)

        @block.scalar
        def _(act):
            def copy_qkv(n, par):
                act.wait_ge(q_ps, n + 1)
                if some(2 * (n - 1)):
                    act.wait_ge(o_ps, 2 * (n - 1))
                act.activation(qT[:, par, :], b_q[:, :], ACT.Copy).then_inc(q_ready, 1)
                if some(n):
                    act.wait_ge(norms_ps, n)
                act.activation(q_sq[:, :], b_q[:, :], ACT.Square).then_inc(q_sq_ready, 1)
                act.wait_ge(k_ps, n + 1)
                act.activation(kT[:, par, :], b_k[:, :], ACT.Copy).then_inc(k_ready, 1)
                act.activation(k_sq[:, :], b_k[:, :], ACT.Square).then_inc(k_sq_ready, 1)
                act.wait_ge(v_ps, n + 1)
                act.activation(v1[:, par, :, :, 0:DH].rearrange("p c h e -> p (c h) e"),
                               b_v[:, :].rearrange("p (c e) -> p c e", e=DH), ACT.Copy).then_inc(v_ready, 1)

            def copy_k_tok(n):
                act.wait_ge(k_tok_ps, n + 1)
                if some(n):
                    act.wait_ge(state_ps, n)
                act.activation(k_tok[:, :, :].rearrange("p c f -> p (c f)"), b_k[:, 0:3 * P], ACT.Copy)\
                    .then_inc(k_tok_ready, 1)

            def copy_oT(u):
                act.wait_ge(oT_ps, u + 1)
                if some(u):
                    act.wait_ge(y_part, u)
                act.activation(oT[:, :], b_oT[:, :], ACT.Copy).then_inc(oT_ready, 1)

            def copy_xnT(b):
                act.wait_ge(xnT_ps, b + 1)
                if some(b * NP):
                    act.wait_ge(v_ps, b * NP)
                if some(b * NF):
                    act.wait_ge(up_ps, b * NF)
                act.activation(xnT[:, :], b_x[:, :], ACT.Copy).then_inc(xnT_ready, 1)

            def silu_hidden(b, f):
                act.wait_ge(gate_h_ps, b * NF + f + 1)
                if some(b * NF + f):
                    act.wait_ge(hidden_ready, b * NF + f)
                act.activation(silu_gate[:, :], b_x[:, :], ACT.Silu).then_inc(silu_h_ready, 1)

            act.wait_ge(pool_const, 11)
            copy_xnT(0)
            copy_qkv(0, 0)
            copy_k_tok(0)

            def body(b, first, last):
                for t in range(NP):
                    u = b * NP + t
                    more = not (last and t == NP - 1)
                    if t < 2:
                        silu_hidden(b, t)
                    if t == 3:
                        act.wait_ge(ffn_ps, b + 1)
                        if some(b):
                            act.wait_ge(mixed_ready, b)
                        act.activation(gate[:, :], b_x[:, :], ACT.Silu).then_inc(gate_ready, 1)
                    if more:
                        copy_qkv(u + 1, (t + 1) % 2)
                    if t == 2:
                        silu_hidden(b, 2)
                    if more:
                        copy_k_tok(u + 1)
                    if t == 6 and not last:
                        copy_xnT(b + 1)
                    copy_oT(u)

            batches(act, body)

        @block.vector
        def _(dve):
            def ln_moments(b):
                dve.wait_ge(x_loaded, 16 * (b + 1))
                for c in range(C):
                    dve.bn_stats(ln_stats[:, c, :], x_in[:, c, :]).then_inc(stats_done, 1)
                dve.wait_ge(stats_done, (b + 1) * C)
                dve.tensor_tensor(ln_gap[:, :], ln_stats[:, :, 1], ln_stats[:, :, 4], ALU.subtract)\
                    .then_inc(moment_step, 1)
                dve.tensor_tensor(ln_sum[:, :], ln_stats[:, :, 1], ln_stats[:, :, 4], ALU.add)\
                    .then_inc(moment_step, 1)
                dve.tensor_tensor(ln_dev[:, :], ln_stats[:, :, 2], ln_stats[:, :, 5], ALU.add)\
                    .then_inc(moment_step, 1)
                dve.wait_ge(moment_step, 5 * b + 3)
                dve.scalar_tensor_tensor(out=ln_gap2[:, :], in0=ln_gap[:, :], scalar=0.25, in1=ln_gap[:, :],
                                         op0=ALU.mult, op1=ALU.mult).then_inc(moment_step, 1)
                dve.tensor_scalar(ln_dev2[:, :], ln_dev[:, :], 1.0 / D, LN_EPS, ALU.mult, ALU.add)\
                    .then_inc(moment_step, 1)
                dve.tensor_scalar(ln_mean[:, :], ln_sum[:, :], 0.5, None, ALU.mult).then_inc(mean_ready, 1)
                dve.wait_ge(moment_step, 5 * b + 5)
                dve.tensor_tensor(ln_var[:, :], ln_dev2[:, :], ln_gap2[:, :], ALU.add).then_inc(var_ready, 1)

            def ln_apply(b):
                dve.wait_ge(rstd_ready, b + 1)
                dve.wait_ge(mean_ready, b + 1)
                if some(b):
                    dve.wait_ge(xnT_ps, b)
                for c in range(C):
                    last = dve.tensor_scalar(xn[:, c, :], x_in[:, c, :], ln_mean[:, c:c + 1], ln_rstd[:, c:c + 1],
                                             ALU.subtract, ALU.mult)
                last.then_inc(xn_ready, 1)

            def past_values(u, par):
                dve.wait_ge(a_ready, u + 1)
                dve.wait_ge(v_sum_ready, u + 1)
                dve.wait_ge(v_ready, u + 1)
                for h in range(2):
                    dve.tensor_scalar(v_past[:, 0, h], v1[:, par, 0, h], a[:, h:h + 1], None, ALU.mult)
                    last = dve.tensor_scalar(v_past[:, 1:3, h], v_sum[:, :, h], a[:, h:h + 1], None, ALU.mult)
                last.then_inc(v_past_ready, 1)

            def make_weights(u):
                for h in range(2):
                    dve.wait_ge(scores_ps, 2 * u + h + 1)
                    dve.scalar_tensor_tensor(out=weights[:, h].rearrange("p c q -> p (c q)"), in0=b_s[h][:, :],
                                             scalar=a[:, h:h + 1], in1=causal[:, :, :].rearrange("p c q -> p (c q)"),
                                             op0=ALU.add, op1=ALU.mult).then_inc(weights_ready, 1)

            def normalise(u):
                for i in range(2):
                    dve.wait_ge(o_ps, 2 * u + i + 1)
                    dve.reciprocal(rden[:, 2 * i:2 * i + 2], o_bank(i)[:, :, :, DH:VE]).then_inc(rden_ready, 1)
                if some(u):
                    dve.wait_ge(oT_ps, u)
                for i in range(2):
                    dve.wait_ge(rden_ready, 2 * u + i + 1)
                    dve.tensor_tensor(o[:, 2 * i:2 * i + 2], o_bank(i)[:, :, :, 0:DH],
                                      rden[:, 2 * i:2 * i + 2].to_broadcast([P, 2, 2, DH]), ALU.mult)\
                        .then_inc(o_ready, 1)

            def reduce_norms(n):
                dve.wait_ge(norms_ps, n + 1)
                dve.tensor_reduce(norm_max[:, :], b_q[0:64, :], AX.X, ALU.max).then_inc(norm_max_ready, 1)
                dve.wait_ge(norm_max_ready, n + 1)
                if some(n):
                    dve.wait_ge(nb_ready, n)
                dve.tensor_scalar(norm_cols[:, :], norm_pick[:, :], norm_max[:, :], None, ALU.mult)\
                    .then_inc(norm_cols_ready, 1)

            def sum_states(n):
                dve.wait_ge(state_ps, n + 1)
                for c in range(3):
                    if c:
                        dve.wait_ge(state_part, 6 * n + 2 * c)
                    for h in range(2):
                        rows = slice(h * DH, (h + 1) * DH)
                        if c == 0:
                            ins = dve.tensor_copy(state[rows, 0, h], st_ps[rows, 0])
                        else:
                            ins = dve.tensor_tensor(state[rows, c, h], st_ps[rows, c], state[rows, c - 1, h], ALU.add)
                        ins.then_inc(state_part, 1)

            def copy_norms(n):
                dve.wait_ge(nb_ready, n + 1)
                dve.wait_ge(state_ps, n + 1)
                if some(n):
                    dve.wait_ge(a_ready, n)
                dve.tensor_copy(norm_sq[:, :], nb_ps).then_inc(norm_sq_ready, 1)

            def mix(b):
                dve.wait_ge(y_part, (b + 1) * NP)
                dve.wait_ge(gate_ready, b + 1)
                if some(b):
                    dve.wait_ge(final_ps, b)
                dve.scalar_tensor_tensor(out=mixed[:, :], in0=b_y[:, :], scalar=bo_col[:, :], in1=gate[:, :],
                                         op0=ALU.add, op1=ALU.mult).then_inc(mixed_ready, 1)

            def add_residual(b):
                dve.wait_ge(final_ps, b + 1)
                dve.wait_ge(x_res_ready, b + 1)
                if some(16 * b):
                    dve.wait_ge(out_stored, 16 * b)
                dve.tensor_tensor(out_sb[:, :, :].rearrange("p c d -> p (c d)"), b_x[:, :],
                                  x_res[:, :, :].rearrange("p c d -> p (c d)"), ALU.add).then_inc(out_ready, 1)

            def keep_x(b):
                if some(b):
                    dve.wait_ge(out_ready, b)
                dve.tensor_copy(x_res[:, :, :], x_in[:, :, :]).then_inc(x_res_ready, 1)

            def multiply_up(b, f):
                dve.wait_ge(up_ps, b * NF + f + 1)
                if some(b):
                    dve.wait_ge(ffn_ps, b)
                dve.tensor_tensor(hidden[:, f, :], b_x[:, :], silu_gate[:, :], ALU.mult)\
                    .then_inc(hidden_ready, 1)

            ln_moments(0)
            ln_apply(0)
            dve.wait_ge(weights_in, 16 * 8)
            for dst, src in ((wg[:, :], wg_i[:, :]), (wu[:, :], wu_i[:, :]), (wd[:, :, :], wd_i[:, :, :])):
                dve.tensor_scalar(dst, src, DEQUANT, None, ALU.mult).then_inc(ffn_w_ready, 1)
            dve.wait_ge(pool_const, 11)
            reduce_norms(0)
            copy_norms(0)
            sum_states(0)

            def body(b, first, last):
                for t in range(NP):
                    u = b * NP + t
                    more = not (last and t == NP - 1)
                    past_values(u, t % 2)
                    make_weights(u)
                    if t == 0 and not first:
                        mix(b - 1)
                    if t == 2 and not first:
                        add_residual(b - 1)
                    if t == 3:
                        keep_x(b)
                    if t == 4 and not last:
                        ln_moments(b + 1)
                    if t == 5 and not last:
                        ln_apply(b + 1)
                    normalise(u)
                    if more:
                        reduce_norms(u + 1)
                    if t < NF:
                        multiply_up(b, t)
                    if more:
                        copy_norms(u + 1)
                        sum_states(u + 1)

            batches(dve, body)
            mix(NB - 1)
            add_residual(NB - 1)


def kernel(L0_attn_X, L0_attn_Wq, L0_attn_Wk, L0_attn_Wv, L0_attn_Wo, L0_attn_bo,
           L0_ffn_w_gate, L0_ffn_w_up, L0_ffn_w_down):
    import numpy as np
    import concourse.bacc as bacc
    from concourse.bass_utils import run_bass_kernel_spmd

    arrays = {
        "X": np.ascontiguousarray(L0_attn_X),
        "WqT": np.ascontiguousarray(np.asarray(L0_attn_Wq).T),
        "WkT": np.ascontiguousarray(np.asarray(L0_attn_Wk).T),
        "WvT": np.ascontiguousarray(np.asarray(L0_attn_Wv).T),
        "WoT": np.ascontiguousarray(np.asarray(L0_attn_Wo).T),
        "bo": np.ascontiguousarray(L0_attn_bo),
        "WgT": np.ascontiguousarray(np.asarray(L0_ffn_w_gate).T),
        "WuT": np.ascontiguousarray(np.asarray(L0_ffn_w_up).T),
        "WdT": np.ascontiguousarray(np.asarray(L0_ffn_w_down).T),
    }
    nc = bacc.Bacc("TRN2", target_bir_lowering=False, num_devices=1)
    args = [nc.dram_tensor(n, v.shape, mybir.dt.from_np(v.dtype), kind="ExternalInput").ap()
            for n, v in arrays.items()]
    out = nc.dram_tensor("out", arrays["X"].shape, F32, kind="ExternalOutput").ap()
    build(nc, *args, out)
    result = run_bass_kernel_spmd(nc, [arrays], core_ids=[0])
    return result.results[0]["out"]
```

```python
from contextlib import ExitStack

import concourse.bass as bass
from concourse import mybir

ALU = mybir.AluOpType
ACT = mybir.ActivationFunctionType
AX = mybir.AxisListType
F32 = mybir.dt.float32
F32R = mybir.dt.float32r
F16 = mybir.dt.float16
I32 = mybir.dt.int32

P = 128
DH = 64
VE = DH + 1
LN_EPS = 1e-5
DEQUANT = 1.0 / 127.0
X_SCALE = 64.0
V_LOG = 9
V_SCALE = 2.0 ** V_LOG
W_SCALE = 256.0


def build(nc, X, WqT, WkT, WvT, WoT, bo, WgT, WuT, WdT, out):
    NB, N, D = X.shape
    HD = WqT.shape[1]
    FF = WgT.shape[1]
    C = N // P
    NP = HD // P
    NF = FF // P
    assert D == P and N == C * P and C == 4 and NP == 8 and NF == 3

    x_dram = X.rearrange("b (c p) d -> b p c d", p=P)
    out_dram = out.rearrange("b (c p) d -> b p c d", p=P)

    with ExitStack() as ctx:
        def sb(name, shape, dt=F32):
            return ctx.enter_context(nc.sbuf_tensor(name, shape, dt))

        def pb(name):
            return ctx.enter_context(nc.psum_tensor(name, [P, 512], F32))

        def sem(name):
            return ctx.enter_context(nc.semaphore(name))

        wq = sb("wq", [P, HD])
        wk = sb("wk", [P, HD])
        wv = sb("wv", [P, HD])
        wo = sb("wo", [P, NP, D])
        bo_col = sb("bo_col", [P, 1])
        wg_i = sb("wg_i", [P, FF], I32)
        wu_i = sb("wu_i", [P, FF], I32)
        wd_i = sb("wd_i", [P, NF, D], I32)
        wg = sb("wg", [P, FF])
        wu = sb("wu", [P, FF])
        wd = sb("wd", [P, NF, D])
        wv_s = sb("wv_s", [P, HD])
        wo_s = sb("wo_s", [P, NP, D])
        wq_p = [sb(f"wq_{x}", [P, HD], F32R) for x in ("hi", "lo")]
        wk_p = [sb(f"wk_{x}", [P, HD], F32R) for x in ("hi", "lo")]
        wv_p = [sb(f"wv_{x}", [P, HD], F16) for x in ("hi", "lo")]
        wo_p = [sb(f"wo_{x}", [P, NP, D], F32R) for x in ("hi", "lo")]
        wg_p = [sb(f"wg_{x}", [P, FF], F32R) for x in ("hi", "lo")]
        wu_p = [sb(f"wu_{x}", [P, FF], F32R) for x in ("hi", "lo")]
        wd_p = [sb(f"wd_{x}", [P, NF, D], F32R) for x in ("hi", "lo")]
        wv_sq = sb("wv_sq", [P, HD])
        row_sq = sb("row_sq", [P, HD])
        exp_sq = sb("exp_sq", [P, HD], I32)
        exp_biased = sb("exp_biased", [P, HD], I32)
        exp_half = sb("exp_half", [P, HD], I32)
        exp_down = sb("exp_down", [P, HD], I32)
        exp_up = sb("exp_up", [P, HD], I32)
        scale_down = sb("scale_down", [P, HD], I32)
        scale_up = sb("scale_up", [P, HD], I32)
        up_col = sb("up_col", [P, NP])
        ident = sb("ident", [P, P])
        ones = sb("ones", [P, P])
        w_ones = sb("w_ones", [P, P], F16)
        causal = sb("causal", [P, P])
        head_sum = sb("head_sum", [P, 32])
        norm_pick = sb("norm_pick", [P, 4])
        head_rows = sb("head_rows", [P, P])
        minus_half = sb("minus_half", [P, C])
        x_in = sb("x_in", [P, C, D])
        x_res = sb("x_res", [P, C, D])
        ln_stats = sb("ln_stats", [P, C, 6])
        ln_sum = sb("ln_sum", [P, C])
        ln_gap = sb("ln_gap", [P, C])
        ln_dev = sb("ln_dev", [P, C])
        ln_gap2 = sb("ln_gap2", [P, C])
        ln_dev2 = sb("ln_dev2", [P, C])
        ln_mean = sb("ln_mean", [P, C])
        ln_var = sb("ln_var", [P, C])
        ln_rstd = sb("ln_rstd", [P, C])
        xn = sb("xn", [P, C, D])
        xr_hi = sb("xr_hi", [P, N], F32R)
        xr_lo = sb("xr_lo", [P, N], F32R)
        xh_hi = sb("xh_hi", [P, N], F16)
        xh_lo = sb("xh_lo", [P, N], F16)
        silu_gate = sb("silu_gate", [P, N])
        hidden = sb("hidden", [P, N])
        hid_hi = sb("hid_hi", [P, NF, N], F32R)
        hid_lo = sb("hid_lo", [P, NF, N], F32R)
        gate = sb("gate", [P, N])
        mixed = sb("mixed", [P, N])
        out_sb = sb("out_sb", [P, C, D])
        qT = sb("qT", [P, N])
        q_norm = sb("q_norm", [P, N])
        kT = sb("kT", [P, N])
        v1 = sb("v1", [P, C, 2, VE])
        v_hi = sb("v_hi", [P, 2, C, 2, VE], F16)
        v_lo = sb("v_lo", [P, 2, C, 2, VE], F16)
        v_sum = sb("v_sum", [P, 2, 2, VE])
        sum_hi = sb("sum_hi", [P, 2, 2, VE], F16)
        sum_lo = sb("sum_lo", [P, 2, 2, VE], F16)
        q_sq = sb("q_sq", [P, N])
        k_sq = sb("k_sq", [P, N])
        k_tok = sb("k_tok", [P, 3, P])
        state = sb("state", [P, 3, 2, VE])
        weights = sb("weights", [P, 2, C, P])
        w_hi = sb("w_hi", [P, 2, C, P], F16)
        w_lo = sb("w_lo", [P, 2, C, P], F16)
        norm_max = sb("norm_max", [P, 1])
        norm_cols = sb("norm_cols", [P, 4])
        norm_sq = sb("norm_sq", [P, 2])
        norm_inv = sb("norm_inv", [P, 2])
        rden = sb("rden", [P, C, 2, 1])
        o = sb("o", [P, C, 2, DH])
        oT_hi = sb("oT_hi", [P, N], F32R)
        oT_lo = sb("oT_lo", [P, N], F32R)

        b_s = [pb("b_s0"), pb("b_s1")]
        b_q = pb("b_q")
        b_k = pb("b_k")
        b_v = pb("b_v")
        b_oT = pb("b_oT")
        b_x = pb("b_x")
        b_y = pb("b_y")

        def o_bank(i):
            return b_s[i][:, 0:4 * VE].rearrange("p (c h e) -> p c h e", c=2, h=2)

        st_ps = b_v[:, 0:3 * VE].rearrange("p (c e) -> p c e", c=3)
        nb_ps = b_q[:, 0:4]

        weights_in = sem("weights_in")
        x_loaded = sem("x_loaded")
        out_stored = sem("out_stored")
        scale_step = sem("scale_step")
        row_sq_ps = sem("row_sq_ps")
        scale_up_ps = sem("scale_up_ps")
        w_scaled = sem("w_scaled")
        w_hi_ready = sem("w_hi_ready")
        w_lo_ready = sem("w_lo_ready")
        v_pad_ready = sem("v_pad_ready")
        pool_const = sem("pool_const")
        zero_fill = sem("zero_fill")
        stats_done = sem("stats_done")
        moment_step = sem("moment_step")
        mean_ready = sem("mean_ready")
        var_ready = sem("var_ready")
        rstd_ready = sem("rstd_ready")
        xn_ready = sem("xn_ready")
        xnT_ps = sem("xnT_ps")
        xr_hi_ready = sem("xr_hi_ready")
        xh_hi_ready = sem("xh_hi_ready")
        x_lo_ready = sem("x_lo_ready")
        x_res_ready = sem("x_res_ready")
        q_ps = sem("q_ps")
        q_ready = sem("q_ready")
        q_sq_ready = sem("q_sq_ready")
        k_ps = sem("k_ps")
        k_ready = sem("k_ready")
        k_sq_ready = sem("k_sq_ready")
        v_ps = sem("v_ps")
        v_hi_ready = sem("v_hi_ready")
        v_lo_ready = sem("v_lo_ready")
        v1_ready = sem("v1_ready")
        v_sum_a = sem("v_sum_a")
        v_sum_ready = sem("v_sum_ready")
        sum_hi_ready = sem("sum_hi_ready")
        sum_lo_ready = sem("sum_lo_ready")
        norms_ps = sem("norms_ps")
        norm_max_ready = sem("norm_max_ready")
        norm_cols_ready = sem("norm_cols_ready")
        nb_ready = sem("nb_ready")
        norm_sq_ready = sem("norm_sq_ready")
        norm_inv_ready = sem("norm_inv_ready")
        q_norm_ready = sem("q_norm_ready")
        k_tok_ps = sem("k_tok_ps")
        k_tok_ready = sem("k_tok_ready")
        state_ps = sem("state_ps")
        state_part = sem("state_part")
        scores_ps = sem("scores_ps")
        weights_ready = sem("weights_ready")
        w16_hi_ready = sem("w16_hi_ready")
        w16_lo0_ready = sem("w16_lo0_ready")
        w16_lo1_ready = sem("w16_lo1_ready")
        o_ps = sem("o_ps")
        rden_ready = sem("rden_ready")
        o_ready = sem("o_ready")
        oT_ps = sem("oT_ps")
        oT_hi_ready = sem("oT_hi_ready")
        oT_lo_ready = sem("oT_lo_ready")
        y_part = sem("y_part")
        mixed_ready = sem("mixed_ready")
        gate_h_ps = sem("gate_h_ps")
        silu_h_ready = sem("silu_h_ready")
        up_ps = sem("up_ps")
        hidden_ready = sem("hidden_ready")
        hid_hi_ready = sem("hid_hi_ready")
        hid_lo_ready = sem("hid_lo_ready")
        ffn_ps = sem("ffn_ps")
        gate_ready = sem("gate_ready")
        final_ps = sem("final_ps")
        out_ready = sem("out_ready")

        def some(count):
            return not isinstance(count, int) or count > 0

        def batches(eng, body):
            body(0, True, False)
            with eng.Fori(1, NB - 1) as b:
                body(b, False, False)
            body(NB - 1, False, True)

        block = ctx.enter_context(nc.Block())

        @block.sync
        def _(sp):
            def load_x(b):
                sp.dma_start(x_in[:, :, :], x_dram[b]).then_inc(x_loaded, 16)

            def store(b):
                sp.wait_ge(out_ready, b + 1)
                sp.dma_start(out_dram[b], out_sb[:, :, :]).then_inc(out_stored, 16)

            load_x(0)
            for dst, src in ((wq[:, :], WqT), (wk[:, :], WkT), (wv[:, :], WvT),
                             (wg_i[:, :], WgT), (wu_i[:, :], WuT)):
                sp.dma_start(dst, src).then_inc(weights_in, 16)
            sp.dma_start(wd_i[:, :, :], WdT.rearrange("(t p) d -> p t d", p=P)).then_inc(weights_in, 16)
            sp.dma_start(wo[:, :, :], WoT.rearrange("(t p) d -> p t d", p=P)).then_inc(weights_in, 16)
            sp.dma_start(bo_col[:, :], bo.rearrange("(p o) -> p o", o=1)).then_inc(weights_in, 16)

            def body(b, first, last):
                if not first:
                    store(b - 1)
                if not last:
                    sp.wait_ge(x_res_ready, b + 1)
                    sp.wait_ge(xn_ready, b + 1)
                    load_x(b + 1)

            batches(sp, body)
            store(NB - 1)
            sp.wait_ge(out_stored, 16 * NB)

        @block.gpsimd
        def _(pool):
            pool.memset(ident[:, :], 0.0).then_inc(zero_fill, 1)
            pool.memset(causal[:, :], 1.0).then_inc(zero_fill, 1)
            pool.memset(head_sum[:, :], 0.0).then_inc(zero_fill, 1)
            pool.memset(norm_pick[:, :], 0.0).then_inc(zero_fill, 1)
            pool.memset(head_rows[:, :], 0.0).then_inc(zero_fill, 1)
            pool.memset(ones[:, :], 1.0).then_inc(pool_const, 1)
            pool.memset(minus_half[:, :], -0.5).then_inc(pool_const, 1)
            pool.wait_ge(zero_fill, 5)
            pool.affine_select(out=ident[:, :], in_=ident[:, :], compare_op=ALU.not_equal, fill=1.0, base=0,
                               pattern=[[-1, P]], channel_multiplier=1).then_inc(pool_const, 1)
            pool.affine_select(out=causal[:, :], in_=causal[:, :], compare_op=ALU.is_ge, fill=0.0, base=0,
                               pattern=[[1, P]], channel_multiplier=-1).then_inc(pool_const, 1)
            for h in range(2):
                pool.wait_ge(pool_const, 4 + h)
                pool.memset(head_sum[h * DH:(h + 1) * DH, h:h + 1], 1.0).then_inc(pool_const, 1)
            for g in range(4):
                quadrant = slice(32 * g, 32 * g + 32)
                pool.wait_ge(pool_const, 6 + 3 * g)
                pool.memset(norm_pick[quadrant, g:g + 1], W_SCALE ** -2 if g < 2 else 1.0).then_inc(pool_const, 1)
                for h in range(2):
                    cols = head_rows[quadrant, h * DH:(h + 1) * DH]
                    pool.affine_select(out=cols, in_=cols, compare_op=ALU.not_equal, fill=1.0, base=-h,
                                       pattern=[[0, DH]], channel_multiplier=1).then_inc(pool_const, 1)
            pool.wait_ge(pool_const, 18)
            pool.memset(state[:, :, :, :], 0.0).then_inc(pool_const, 1)
            pool.memset(w_ones[:, :], W_SCALE).then_inc(pool_const, 1)
            pool.memset(v1[:, :, :, :], 1.0).then_inc(v_pad_ready, 1)
            pool.memset(v_hi[:, :, :, :, :], 1.0).then_inc(v_pad_ready, 1)
            pool.memset(v_lo[:, :, :, :, :], 0.0).then_inc(v_pad_ready, 1)

            def ln_rstd_of(b):
                pool.wait_ge(var_ready, b + 1)
                pool.tensor_tensor(ln_rstd[:, :], ln_var[:, :], minus_half[:, :], ALU.pow).then_inc(rstd_ready, 1)

            def value_sums(n):
                pool.wait_ge(v1_ready, n + 1)
                if some(n):
                    pool.wait_ge(sum_hi_ready, n)
                    pool.wait_ge(sum_lo_ready, n)
                pool.tensor_tensor(v_sum[:, 0], v1[:, 0], v1[:, 1], ALU.add).then_inc(v_sum_a, 1)
                pool.wait_ge(v_sum_a, n + 1)
                pool.tensor_tensor(v_sum[:, 1], v_sum[:, 0], v1[:, 2], ALU.add).then_inc(v_sum_ready, 1)

            def value_sums_lo(n):
                pool.wait_ge(sum_hi_ready, n + 1)
                if some(n):
                    pool.wait_ge(o_ps, 2 * n)
                pool.tensor_tensor(sum_lo[:, :, :, :], v_sum[:, :, :, :], sum_hi[:, :, :, :], ALU.subtract)\
                    .then_inc(sum_lo_ready, 1)

            def weights_lo0(u):
                pool.wait_ge(w16_hi_ready, 2 * u + 1)
                if some(2 * u):
                    pool.wait_ge(o_ps, 2 * u)
                pool.tensor_tensor(w_lo[:, 0], weights[:, 0], w_hi[:, 0], ALU.subtract).then_inc(w16_lo0_ready, 1)

            def invert_norms(n):
                pool.wait_ge(norm_sq_ready, n + 1)
                if some(n):
                    pool.wait_ge(q_norm_ready, n)
                pool.tensor_tensor(norm_inv[:, :], norm_sq[:, :], minus_half[:, 0:2], ALU.pow)\
                    .then_inc(norm_inv_ready, 1)

            def values_lo(n, par):
                pool.wait_ge(v_hi_ready, n + 1)
                pool.wait_ge(v1_ready, n + 1)
                if some(2 * n - 2):
                    pool.wait_ge(o_ps, 2 * n - 2)
                pool.tensor_tensor(v_lo[:, par, :, :, 0:DH].rearrange("p c h e -> p (c h) e"),
                                   v1[:, :, :, 0:DH].rearrange("p c h e -> p (c h) e"),
                                   v_hi[:, par, :, :, 0:DH].rearrange("p c h e -> p (c h) e"),
                                   ALU.subtract).then_inc(v_lo_ready, 1)

            pool.wait_ge(pool_const, 20)
            pool.wait_ge(v_pad_ready, 3)
            ln_rstd_of(0)
            invert_norms(0)
            value_sums(0)
            values_lo(0, 0)
            value_sums_lo(0)

            def body(b, first, last):
                for t in range(NP):
                    u = b * NP + t
                    weights_lo0(u)
                    if t == 5 and not last:
                        ln_rstd_of(b + 1)
                    if not (last and t == NP - 1):
                        value_sums(u + 1)
                        invert_norms(u + 1)
                        values_lo(u + 1, (t + 1) % 2)
                        value_sums_lo(u + 1)

            batches(pool, body)

        @block.tensor
        def _(pe):
            def split_product(out_ps, stationary, moving, start=True, stop=True):
                (s_hi, s_lo), (m_hi, m_lo) = stationary, moving
                pe.matmul(out_ps, s_hi, m_hi, start=start, stop=False, skip_group_check=True)
                pe.matmul(out_ps, s_hi, m_lo, start=False, stop=False, skip_group_check=True)
                return pe.matmul(out_ps, s_lo, m_hi, start=False, stop=stop, skip_group_check=True)

            def tile(parts, t):
                return [w[:, t * P:(t + 1) * P] for w in parts]

            xr = (xr_hi[:, :], xr_lo[:, :])

            def project_qk(n, t):
                if some(n):
                    pe.wait_ge(norm_sq_ready, n)
                    pe.wait_ge(q_ready, n)
                split_product(b_q[:, :], tile(wq_p, t), xr).then_inc(q_ps, 1)
                if some(n):
                    pe.wait_ge(k_tok_ready, n)
                split_product(b_k[:, :], tile(wk_p, t), xr).then_inc(k_ps, 1)

            def project_v(n, t):
                if some(6 * n):
                    pe.wait_ge(state_part, 6 * n)
                for c in range(C):
                    mm = split_product(b_v[:, c * P:(c + 1) * P], tile((xh_hi, xh_lo), c), tile(wv_p, t))
                mm.then_inc(v_ps, 1)

            def norms(n):
                pe.wait_ge(q_ready, n + 1)
                pe.wait_ge(q_sq_ready, n + 1)
                for g in range(2):
                    pe.matmul(b_q[32 * g:32 * g + 32, 0:N // 2], head_sum[:, :],
                              q_sq[:, g * (N // 2):(g + 1) * (N // 2)], start=True, stop=True)
                pe.wait_ge(k_sq_ready, n + 1)
                for g in range(2, 4):
                    mm = pe.matmul(b_q[32 * g:32 * g + 32, 0:N // 2], head_sum[:, :],
                                   k_sq[:, (g - 2) * (N // 2):(g - 1) * (N // 2)], start=True, stop=True)
                mm.then_inc(norms_ps, 1)

            def keys_by_token(n):
                pe.wait_ge(k_ready, n + 1)
                pe.wait_ge(k_sq_ready, n + 1)
                for c in range(3):
                    mm = pe.transpose(b_k[:, c * P:(c + 1) * P], kT[:, c * P:(c + 1) * P], ident[:, :])
                mm.then_inc(k_tok_ps, 1)

            def states(n):
                pe.wait_ge(k_tok_ready, n + 1)
                pe.wait_ge(v1_ready, n + 1)
                for c in range(3):
                    for h in range(2):
                        mm = pe.matmul(st_ps[h * DH:(h + 1) * DH, c], k_tok[:, c, h * DH:(h + 1) * DH],
                                       v1[:, c, h, :], start=True, stop=True)
                mm.then_inc(state_ps, 1)

            def spread_norms(n):
                pe.wait_ge(norm_cols_ready, n + 1)
                pe.matmul(nb_ps, head_rows[:, :], norm_cols[:, :], start=True, stop=True).then_inc(nb_ready, 1)

            def scores(u):
                pe.wait_ge(q_norm_ready, u + 1)
                pe.wait_ge(k_ready, u + 1)
                if some(2 * u):
                    pe.wait_ge(o_ready, 2 * u)
                for h in range(2):
                    for c in range(C):
                        rows = slice(h * DH, (h + 1) * DH)
                        mm = pe.matmul(b_s[h][:, c * P:(c + 1) * P], kT[rows, c * P:(c + 1) * P],
                                       q_norm[rows, c * P:(c + 1) * P], start=True, stop=True)
                    mm.then_inc(scores_ps, 1)

            def attend_before(u, par):
                pe.wait_ge(weights_ready, 2 * u + 2)
                pe.wait_ge(v_hi_ready, u + 1)
                pe.wait_ge(v_lo_ready, u + 1)
                pe.wait_ge(sum_lo_ready, u + 1)
                pe.matmul(o_bank(0)[:, 1], w_ones[:, :], v_hi[:, par, 0], start=True, stop=False,
                          skip_group_check=True)
                pe.matmul(o_bank(0)[:, 1], w_ones[:, :], v_lo[:, par, 0], start=False, stop=False,
                          skip_group_check=True)
                pe.matmul(o_bank(1), w_ones[:, :], sum_hi[:, :, :, :], start=True, stop=False,
                          skip_group_check=True)
                pe.matmul(o_bank(1), w_ones[:, :], sum_lo[:, :, :, :], start=False, stop=False,
                          skip_group_check=True)
                pe.wait_ge(state_part, 6 * (u + 1))
                for c in range(1, C):
                    pe.matmul(o_bank(c // 2)[:, c % 2], q_norm[:, c * P:(c + 1) * P], state[:, c - 1],
                              start=False, stop=False, skip_group_check=True)

            def attend_own(u, par):
                pe.wait_ge(w16_lo0_ready, u + 1)
                pe.wait_ge(w16_lo1_ready, u + 1)
                for i in range(2):
                    for c in range(2 * i, 2 * i + 2):
                        for h in range(2):
                            mm = split_product(o_bank(i)[:, c % 2, h], (w_hi[:, h, c], w_lo[:, h, c]),
                                               (v_hi[:, par, c, h, :], v_lo[:, par, c, h, :]), start=False)
                    mm.then_inc(o_ps, 1)

            def turn_outputs(u):
                pe.wait_ge(o_ready, 2 * (u + 1))
                if some(u):
                    pe.wait_ge(oT_lo_ready, u)
                for c in range(C):
                    mm = pe.transpose(b_oT[:, c * P:(c + 1) * P], o[:, c].rearrange("p h e -> p (h e)"), ident[:, :])
                mm.then_inc(oT_ps, 1)

            def project_out(u, t, mixed_before):
                pe.wait_ge(oT_hi_ready, u + 1)
                pe.wait_ge(oT_lo_ready, u + 1)
                if t == 0:
                    if some(mixed_before):
                        pe.wait_ge(mixed_ready, mixed_before)
                split_product(b_y[:, :], [w[:, t, :] for w in wo_p], (oT_hi[:, :], oT_lo[:, :]),
                              start=(t == 0), stop=(t == NP - 1)).then_inc(y_part, 1)

            def ffn_gate(b, f):
                if f == 0:
                    if some(b):
                        pe.wait_ge(gate_ready, b)
                else:
                    pe.wait_ge(hidden_ready, b * NF + f)
                split_product(b_x[:, :], tile(wg_p, f), xr).then_inc(gate_h_ps, 1)

            def ffn_up(b, f):
                pe.wait_ge(silu_h_ready, b * NF + f + 1)
                if f == 0 and some(b):
                    pe.wait_ge(out_ready, b)
                split_product(b_x[:, :], tile(wu_p, f), xr).then_inc(up_ps, 1)

            def ffn_down(b, last):
                if not last:
                    pe.wait_ge(xh_hi_ready, b + 2)
                    pe.wait_ge(x_lo_ready, 2 * b + 4)
                pe.wait_ge(hid_hi_ready, b * NF + NF)
                pe.wait_ge(hid_lo_ready, b * NF + NF)
                for f in range(NF):
                    mm = split_product(b_x[:, :], [w[:, f, :] for w in wd_p], (hid_hi[:, f, :], hid_lo[:, f, :]),
                                       start=(f == 0), stop=(f == NF - 1))
                mm.then_inc(ffn_ps, 1)

            def turn_xn(b):
                pe.wait_ge(xn_ready, b + 1)
                if some(b * NF):
                    pe.wait_ge(hidden_ready, b * NF)
                for c in range(C):
                    mm = pe.transpose(b_x[:, c * P:(c + 1) * P], xn[:, c, :], ident[:, :])
                mm.then_inc(xnT_ps, 1)

            def turn_mixed(b, silu_count):
                pe.wait_ge(mixed_ready, b + 1)
                pe.wait_ge(silu_h_ready, silu_count)
                for c in range(C):
                    mm = pe.transpose(b_x[:, c * P:(c + 1) * P], mixed[:, c * P:(c + 1) * P], ident[:, :])
                mm.then_inc(final_ps, 1)

            pe.wait_ge(pool_const, 18)
            pe.wait_ge(scale_step, 1)
            for i, bank in enumerate((b_y, b_oT)):
                mm = pe.matmul(bank[:, :], ones[:, :], wv_sq[:, i * 512:(i + 1) * 512], start=True, stop=True)
            mm.then_inc(row_sq_ps, 1)
            turn_xn(0)
            pe.wait_ge(scale_step, 10)
            for t in range(NP):
                mm = pe.transpose(b_s[t // 4][:, (t % 4) * P:(t % 4 + 1) * P],
                                  scale_up[:, t * P:(t + 1) * P].bitcast(F32), ident[:, :])
            mm.then_inc(scale_up_ps, 1)
            pe.wait_ge(pool_const, 20)
            pe.wait_ge(w_hi_ready, 7)
            pe.wait_ge(w_lo_ready, 7)
            pe.wait_ge(xh_hi_ready, 1)
            pe.wait_ge(x_lo_ready, 2)
            project_qk(0, 0)
            project_v(0, 0)
            norms(0)
            keys_by_token(0)
            spread_norms(0)
            states(0)

            def body(b, first, last):
                for t in range(NP):
                    u = b * NP + t
                    par = t % 2
                    nt = (t + 1) % NP
                    more = not (last and t == NP - 1)
                    scores(u)
                    if more:
                        if t == NP - 1:
                            pe.wait_ge(xh_hi_ready, b + 2)
                            pe.wait_ge(x_lo_ready, 2 * b + 4)
                        project_qk(u + 1, nt)
                        project_v(u + 1, nt)
                    if not (first and t == 0):
                        turn_outputs(u - 1)
                    if t == 1 and not first:
                        turn_mixed(b - 1, b * NF + 1)
                    attend_before(u, par)
                    if more:
                        norms(u + 1)
                        keys_by_token(u + 1)
                    attend_own(u, par)
                    if more:
                        spread_norms(u + 1)
                    if t == 6 and not last:
                        turn_xn(b + 1)
                    if not (first and t == 0):
                        project_out(u - 1, (t - 1) % NP, b)
                    if more:
                        states(u + 1)
                    if t in (0, 2, 4):
                        ffn_gate(b, t // 2)
                    if t in (1, 3, 5):
                        ffn_up(b, t // 2)
                    if t == 7:
                        ffn_down(b, last)

            batches(pe, body)
            turn_outputs(NB * NP - 1)
            project_out(NB * NP - 1, NP - 1, NB - 1)
            pe.wait_ge(gate_ready, NB)
            turn_mixed(NB - 1, NB * NF)

        @block.scalar
        def _(act):
            def split_hi(out, value, ready, scale=1.0):
                act.activation(out, value, ACT.Copy, scale=scale).then_inc(ready, 1)

            def copy_qk(n):
                act.wait_ge(q_ps, n + 1)
                if some(n):
                    act.wait_ge(scores_ps, 2 * n)
                act.activation(qT[:, :], b_q[:, :], ACT.Copy).then_inc(q_ready, 1)
                act.wait_ge(k_ps, n + 1)
                if some(n):
                    act.wait_ge(norms_ps, n)
                act.activation(kT[:, :], b_k[:, :], ACT.Copy).then_inc(k_ready, 1)
                act.activation(q_sq[:, :], b_q[:, :], ACT.Square).then_inc(q_sq_ready, 1)

            def copy_v(n, par):
                act.wait_ge(v_ps, n + 1)
                act.activation(v_hi[:, par, :, :, 0:DH].rearrange("p c h e -> p (c h) e"),
                               b_v[:, :].rearrange("p (c e) -> p c e", e=DH), ACT.Copy, scale=1.0 / X_SCALE)\
                    .then_inc(v_hi_ready, 1)
                if some(n):
                    act.wait_ge(state_ps, n)
                    act.wait_ge(v_sum_ready, n)
                    act.wait_ge(v_lo_ready, n)
                act.activation(v1[:, :, :, 0:DH].rearrange("p c h e -> p (c h) e"),
                               b_v[:, :].rearrange("p (c e) -> p c e", e=DH), ACT.Copy, scale=1.0 / X_SCALE)\
                    .then_inc(v1_ready, 1)

            def copy_k_tok(n):
                act.wait_ge(k_tok_ps, n + 1)
                act.activation(k_tok[:, :, :].rearrange("p c f -> p (c f)"), b_k[:, 0:3 * P], ACT.Copy)\
                    .then_inc(k_tok_ready, 1)

            def value_sums_hi(n):
                act.wait_ge(v_sum_ready, n + 1)
                if some(2 * n):
                    act.wait_ge(o_ps, 2 * n)
                act.activation(sum_hi[:, :, :, :], v_sum[:, :, :, :], ACT.Copy).then_inc(sum_hi_ready, 1)

            def weights_hi(u):
                if some(2 * u):
                    act.wait_ge(o_ps, 2 * u)
                for h in range(2):
                    act.wait_ge(weights_ready, 2 * u + h + 1)
                    act.activation(w_hi[:, h], weights[:, h], ACT.Copy).then_inc(w16_hi_ready, 1)

            def copy_oT(u):
                act.wait_ge(oT_ps, u + 1)
                if some(u):
                    act.wait_ge(y_part, u)
                act.activation(oT_hi[:, :], b_oT[:, :], ACT.Copy).then_inc(oT_hi_ready, 1)

            def copy_xnT(b):
                act.wait_ge(xnT_ps, b + 1)
                if some(b * NP):
                    act.wait_ge(v_ps, b * NP)
                if some(b * NF):
                    act.wait_ge(up_ps, b * NF)
                act.activation(xr_hi[:, :], b_x[:, :], ACT.Copy).then_inc(xr_hi_ready, 1)
                act.activation(xh_hi[:, :], b_x[:, :], ACT.Copy, scale=X_SCALE).then_inc(xh_hi_ready, 1)

            def silu_hidden(b, f):
                act.wait_ge(gate_h_ps, b * NF + f + 1)
                if some(b * NF + f):
                    act.wait_ge(hidden_ready, b * NF + f)
                act.activation(silu_gate[:, :], b_x[:, :], ACT.Silu).then_inc(silu_h_ready, 1)

            def hidden_hi(b, f):
                act.wait_ge(hidden_ready, b * NF + f + 1)
                if some(b):
                    act.wait_ge(ffn_ps, b)
                act.activation(hid_hi[:, f, :], hidden[:, :], ACT.Copy).then_inc(hid_hi_ready, 1)

            act.wait_ge(weights_in, 16 * 8)
            act.activation(wq_p[0][:, :], wq[:, :], ACT.Copy).then_inc(w_hi_ready, 1)
            act.activation(wk_p[0][:, :], wk[:, :], ACT.Copy).then_inc(w_hi_ready, 1)
            copy_xnT(0)
            act.wait_ge(w_scaled, 1)
            act.activation(wv_p[0][:, :], wv_s[:, :], ACT.Copy).then_inc(w_hi_ready, 1)
            act.wait_ge(w_scaled, 4)
            for part, w in ((wg_p[0][:, :], wg[:, :]), (wu_p[0][:, :], wu[:, :]), (wd_p[0][:, :, :], wd[:, :, :])):
                act.activation(part, w, ACT.Copy).then_inc(w_hi_ready, 1)
            act.wait_ge(w_scaled, 12)
            act.activation(wo_p[0][:, :, :], wo_s[:, :, :], ACT.Copy).then_inc(w_hi_ready, 1)
            act.wait_ge(v_pad_ready, 3)
            copy_qk(0)
            copy_v(0, 0)
            copy_k_tok(0)
            value_sums_hi(0)

            def body(b, first, last):
                for t in range(NP):
                    u = b * NP + t
                    more = not (last and t == NP - 1)
                    weights_hi(u)
                    if more:
                        copy_qk(u + 1)
                    if not (first and t == 0):
                        copy_oT(u - 1)
                    if more:
                        copy_v(u + 1, (t + 1) % 2)
                        copy_k_tok(u + 1)
                    if t in (2, 4, 6):
                        hidden_hi(b, t // 2 - 1)
                    if more:
                        value_sums_hi(u + 1)
                    if t == 6 and not last:
                        copy_xnT(b + 1)
                    if t in (0, 2, 4):
                        silu_hidden(b, t // 2)
                    if t == 7:
                        act.wait_ge(ffn_ps, b + 1)
                        if some(b):
                            act.wait_ge(mixed_ready, b)
                        act.activation(gate[:, :], b_x[:, :], ACT.Silu).then_inc(gate_ready, 1)

            batches(act, body)
            copy_oT(NB * NP - 1)

        @block.vector
        def _(dve):
            def ln_moments(b):
                dve.wait_ge(x_loaded, 16 * (b + 1))
                for c in range(C):
                    dve.bn_stats(ln_stats[:, c, :], x_in[:, c, :]).then_inc(stats_done, 1)
                dve.wait_ge(stats_done, (b + 1) * C)
                dve.tensor_tensor(ln_gap[:, :], ln_stats[:, :, 1], ln_stats[:, :, 4], ALU.subtract)\
                    .then_inc(moment_step, 1)
                dve.tensor_tensor(ln_sum[:, :], ln_stats[:, :, 1], ln_stats[:, :, 4], ALU.add)\
                    .then_inc(moment_step, 1)
                dve.tensor_tensor(ln_dev[:, :], ln_stats[:, :, 2], ln_stats[:, :, 5], ALU.add)\
                    .then_inc(moment_step, 1)
                dve.wait_ge(moment_step, 5 * b + 3)
                dve.scalar_tensor_tensor(out=ln_gap2[:, :], in0=ln_gap[:, :], scalar=0.25, in1=ln_gap[:, :],
                                         op0=ALU.mult, op1=ALU.mult).then_inc(moment_step, 1)
                dve.tensor_scalar(ln_dev2[:, :], ln_dev[:, :], 1.0 / D, LN_EPS, ALU.mult, ALU.add)\
                    .then_inc(moment_step, 1)
                dve.tensor_scalar(ln_mean[:, :], ln_sum[:, :], 0.5, None, ALU.mult).then_inc(mean_ready, 1)
                dve.wait_ge(moment_step, 5 * b + 5)
                dve.tensor_tensor(ln_var[:, :], ln_dev2[:, :], ln_gap2[:, :], ALU.add).then_inc(var_ready, 1)

            def ln_apply(b):
                dve.wait_ge(rstd_ready, b + 1)
                dve.wait_ge(mean_ready, b + 1)
                if some(b):
                    dve.wait_ge(xnT_ps, b)
                for c in range(C):
                    last = dve.tensor_scalar(xn[:, c, :], x_in[:, c, :], ln_mean[:, c:c + 1], ln_rstd[:, c:c + 1],
                                             ALU.subtract, ALU.mult)
                last.then_inc(xn_ready, 1)

            def split_xn(b):
                dve.wait_ge(xr_hi_ready, b + 1)
                dve.wait_ge(xh_hi_ready, b + 1)
                dve.tensor_tensor(xr_lo[:, :], b_x[:, :], xr_hi[:, :].bitcast(F32), ALU.subtract)\
                    .then_inc(x_lo_ready, 1)
                dve.scalar_tensor_tensor(out=xh_lo[:, :], in0=b_x[:, :], scalar=X_SCALE, in1=xh_hi[:, :],
                                         op0=ALU.mult, op1=ALU.subtract).then_inc(x_lo_ready, 1)

            def normalise_q(n):
                dve.wait_ge(norm_inv_ready, n + 1)
                dve.wait_ge(q_ready, n + 1)
                if some(2 * n):
                    dve.wait_ge(o_ps, 2 * n)
                dve.tensor_scalar(q_norm[:, :], qT[:, :], norm_inv[:, 0:1], norm_inv[:, 1:2], ALU.mult, ALU.mult)\
                    .then_inc(q_norm_ready, 1)

            def make_weights(u, h):
                dve.wait_ge(scores_ps, 2 * u + h + 1)
                if h == 0 and some(u):
                    dve.wait_ge(w16_lo0_ready, u)
                dve.scalar_tensor_tensor(out=weights[:, h], in0=b_s[h][:, :].rearrange("p (c q) -> p c q", c=C),
                                         scalar=W_SCALE, in1=causal_all, op0=ALU.add, op1=ALU.mult)\
                    .then_inc(weights_ready, 1)

            causal_all = causal[:, :].rearrange("p (o q) -> p o q", o=1).to_broadcast([P, C, P])

            def weights_lo1(u):
                dve.wait_ge(w16_hi_ready, 2 * u + 2)
                if some(2 * u):
                    dve.wait_ge(o_ps, 2 * u)
                dve.tensor_tensor(w_lo[:, 1], weights[:, 1], w_hi[:, 1], ALU.subtract).then_inc(w16_lo1_ready, 1)

            def outputs_lo(u):
                dve.wait_ge(oT_hi_ready, u + 1)
                dve.tensor_tensor(oT_lo[:, :], b_oT[:, :], oT_hi[:, :].bitcast(F32), ALU.subtract)\
                    .then_inc(oT_lo_ready, 1)

            def hidden_lo(b, f):
                dve.wait_ge(hid_hi_ready, b * NF + f + 1)
                dve.tensor_tensor(hid_lo[:, f, :], hidden[:, :], hid_hi[:, f, :].bitcast(F32), ALU.subtract)\
                    .then_inc(hid_lo_ready, 1)

            def normalise(u):
                for i in range(2):
                    dve.wait_ge(o_ps, 2 * u + i + 1)
                    dve.reciprocal(rden[:, 2 * i:2 * i + 2], o_bank(i)[:, :, :, DH:VE]).then_inc(rden_ready, 1)
                if some(u):
                    dve.wait_ge(oT_ps, u)
                for i in range(2):
                    dve.wait_ge(rden_ready, 2 * u + i + 1)
                    dve.tensor_tensor(o[:, 2 * i:2 * i + 2], o_bank(i)[:, :, :, 0:DH],
                                      rden[:, 2 * i:2 * i + 2].to_broadcast([P, 2, 2, DH]), ALU.mult)\
                        .then_inc(o_ready, 1)

            def reduce_norms(n):
                dve.wait_ge(norms_ps, n + 1)
                dve.tensor_reduce(norm_max[:, :], b_q[:, 0:N // 2], AX.X, ALU.max).then_inc(norm_max_ready, 1)
                dve.wait_ge(norm_max_ready, n + 1)
                if some(n):
                    dve.wait_ge(nb_ready, n)
                dve.tensor_scalar(norm_cols[:, :], norm_pick[:, :], norm_max[:, :], None, ALU.mult)\
                    .then_inc(norm_cols_ready, 1)

            def sum_states(n, c):
                if c == 0:
                    dve.wait_ge(state_ps, n + 1)
                else:
                    dve.wait_ge(state_part, 6 * n + 2 * c)
                for h in range(2):
                    rows = slice(h * DH, (h + 1) * DH)
                    if c == 0:
                        ins = dve.tensor_copy(state[rows, 0, h], st_ps[rows, 0])
                    else:
                        ins = dve.tensor_tensor(state[rows, c, h], st_ps[rows, c], state[rows, c - 1, h], ALU.add)
                    ins.then_inc(state_part, 1)

            def copy_norms(n):
                dve.wait_ge(nb_ready, n + 1)
                if some(n):
                    dve.wait_ge(norm_inv_ready, n)
                dve.tensor_reduce(norm_sq[:, :], nb_ps.rearrange("p (j s) -> p j s", s=2), AX.X, ALU.max)\
                    .then_inc(norm_sq_ready, 1)

            def mix(b):
                dve.wait_ge(y_part, (b + 1) * NP)
                dve.wait_ge(gate_ready, b + 1)
                if some(b):
                    dve.wait_ge(final_ps, b)
                dve.scalar_tensor_tensor(out=mixed[:, :], in0=b_y[:, :], scalar=bo_col[:, :], in1=gate[:, :],
                                         op0=ALU.add, op1=ALU.mult).then_inc(mixed_ready, 1)

            def add_residual(b):
                dve.wait_ge(final_ps, b + 1)
                dve.wait_ge(x_res_ready, b + 1)
                if some(16 * b):
                    dve.wait_ge(out_stored, 16 * b)
                dve.tensor_tensor(out_sb[:, :, :].rearrange("p c d -> p (c d)"), b_x[:, :],
                                  x_res[:, :, :].rearrange("p c d -> p (c d)"), ALU.add).then_inc(out_ready, 1)

            def keep_x(b):
                if some(b):
                    dve.wait_ge(out_ready, b)
                dve.tensor_copy(x_res[:, :, :], x_in[:, :, :]).then_inc(x_res_ready, 1)

            def square_k(n):
                dve.wait_ge(k_ready, n + 1)
                if some(n):
                    dve.wait_ge(norms_ps, n)
                dve.tensor_tensor(k_sq[:, :], kT[:, :], kT[:, :], ALU.mult).then_inc(k_sq_ready, 1)

            def multiply_up(b, f):
                dve.wait_ge(up_ps, b * NF + f + 1)
                dve.tensor_tensor(hidden[:, :], b_x[:, :], silu_gate[:, :], ALU.mult)\
                    .then_inc(hidden_ready, 1)

            ln_moments(0)
            dve.wait_ge(weights_in, 16 * 8)
            dve.tensor_tensor(wv_sq[:, :], wv[:, :], wv[:, :], ALU.mult).then_inc(scale_step, 1)
            ln_apply(0)
            dve.wait_ge(row_sq_ps, 1)
            for i, bank in enumerate((b_y, b_oT)):
                dve.tensor_copy(row_sq[:, i * 512:(i + 1) * 512], bank[:, :]).then_inc(scale_step, 1)
            dve.wait_ge(scale_step, 3)
            dve.tensor_scalar(exp_sq[:, :], row_sq[:, :].bitcast(I32), 23, None, ALU.logical_shift_right)\
                .then_inc(scale_step, 1)
            dve.wait_ge(scale_step, 4)
            dve.tensor_scalar(exp_biased[:, :], exp_sq[:, :], 127.0, None, ALU.add).then_inc(scale_step, 1)
            dve.wait_ge(scale_step, 5)
            dve.tensor_scalar(exp_half[:, :], exp_biased[:, :], 1, None, ALU.logical_shift_right)\
                .then_inc(scale_step, 1)
            dve.wait_ge(scale_step, 6)
            dve.tensor_scalar(exp_down[:, :], exp_half[:, :], -1.0, 254.0 + V_LOG, ALU.mult, ALU.add)\
                .then_inc(scale_step, 1)
            dve.tensor_scalar(exp_up[:, :], exp_half[:, :], -1.0 * V_LOG, None, ALU.add).then_inc(scale_step, 1)
            dve.wait_ge(scale_step, 8)
            dve.tensor_scalar(scale_down[:, :], exp_down[:, :], 23, None, ALU.logical_shift_left)\
                .then_inc(scale_step, 1)
            dve.tensor_scalar(scale_up[:, :], exp_up[:, :], 23, None, ALU.logical_shift_left)\
                .then_inc(scale_step, 1)
            dve.wait_ge(scale_step, 10)
            dve.tensor_tensor(wv_s[:, :], wv[:, :], scale_down[:, :].bitcast(F32), ALU.mult).then_inc(w_scaled, 1)
            for dst, src in ((wg[:, :], wg_i[:, :]), (wu[:, :], wu_i[:, :]), (wd[:, :, :], wd_i[:, :, :])):
                dve.tensor_scalar(dst, src, DEQUANT, None, ALU.mult).then_inc(w_scaled, 1)
            dve.wait_ge(scale_up_ps, 1)
            for i in range(2):
                dve.tensor_copy(up_col[:, 4 * i:4 * i + 4], b_s[i][:, :].rearrange("p (t q) -> p t q", t=4)[:, :, 0])\
                    .then_inc(scale_step, 1)
            dve.wait_ge(scale_step, 12)
            for t in range(NP):
                dve.tensor_scalar(wo_s[:, t, :], wo[:, t, :], up_col[:, t:t + 1], None, ALU.mult)\
                    .then_inc(w_scaled, 1)
            for i, (lo, w, hi) in enumerate((
                    (wq_p[1][:, :], wq[:, :], wq_p[0][:, :]), (wk_p[1][:, :], wk[:, :], wk_p[0][:, :]),
                    (wv_p[1][:, :], wv_s[:, :], wv_p[0][:, :]), (wg_p[1][:, :], wg[:, :], wg_p[0][:, :]),
                    (wu_p[1][:, :], wu[:, :], wu_p[0][:, :]), (wd_p[1][:, :, :], wd[:, :, :], wd_p[0][:, :, :]),
                    (wo_p[1][:, :, :], wo_s[:, :, :], wo_p[0][:, :, :]))):
                dve.wait_ge(w_hi_ready, i + 1)
                dve.tensor_tensor(lo, w, hi if i == 2 else hi.bitcast(F32), ALU.subtract).then_inc(w_lo_ready, 1)
                if i == 1:
                    split_xn(0)
            dve.wait_ge(pool_const, 20)
            dve.wait_ge(v_pad_ready, 3)
            square_k(0)
            reduce_norms(0)
            copy_norms(0)
            normalise_q(0)

            def body(b, first, last):
                for t in range(NP):
                    u = b * NP + t
                    more = not (last and t == NP - 1)
                    sum_states(u, 0)
                    make_weights(u, 0)
                    sum_states(u, 1)
                    make_weights(u, 1)
                    sum_states(u, 2)
                    weights_lo1(u)
                    if more:
                        square_k(u + 1)
                    if t in (2, 4, 6):
                        multiply_up(b, t // 2 - 1)
                    if t == 1 and not first:
                        add_residual(b - 1)
                    if t in (3, 5, 7):
                        hidden_lo(b, t // 2 - 1)
                    if not (first and t == 0):
                        outputs_lo(u - 1)
                    if more:
                        reduce_norms(u + 1)
                    if t == 3:
                        keep_x(b)
                    if more:
                        copy_norms(u + 1)
                    normalise(u)
                    if more:
                        normalise_q(u + 1)
                    if t == 4 and not last:
                        ln_moments(b + 1)
                    if t == 5 and not last:
                        ln_apply(b + 1)
                    if t == 6 and not last:
                        split_xn(b + 1)
                    if t == 0 and not first:
                        mix(b - 1)

            batches(dve, body)
            outputs_lo(NB * NP - 1)
            mix(NB - 1)
            add_residual(NB - 1)


def kernel(L0_attn_X, L0_attn_Wq, L0_attn_Wk, L0_attn_Wv, L0_attn_Wo, L0_attn_bo,
           L0_ffn_w_gate, L0_ffn_w_up, L0_ffn_w_down):
    import numpy as np
    import concourse.bacc as bacc
    from concourse.bass_utils import run_bass_kernel_spmd

    arrays = {
        "X": np.ascontiguousarray(L0_attn_X),
        "WqT": np.ascontiguousarray(np.asarray(L0_attn_Wq).T),
        "WkT": np.ascontiguousarray(np.asarray(L0_attn_Wk).T),
        "WvT": np.ascontiguousarray(np.asarray(L0_attn_Wv).T),
        "WoT": np.ascontiguousarray(np.asarray(L0_attn_Wo).T),
        "bo": np.ascontiguousarray(L0_attn_bo),
        "WgT": np.ascontiguousarray(np.asarray(L0_ffn_w_gate).T),
        "WuT": np.ascontiguousarray(np.asarray(L0_ffn_w_up).T),
        "WdT": np.ascontiguousarray(np.asarray(L0_ffn_w_down).T),
    }
    nc = bacc.Bacc("TRN2", target_bir_lowering=False, num_devices=1)
    args = [nc.dram_tensor(n, v.shape, mybir.dt.from_np(v.dtype), kind="ExternalInput").ap()
            for n, v in arrays.items()]
    out = nc.dram_tensor("out", arrays["X"].shape, F32, kind="ExternalOutput").ap()
    build(nc, *args, out)
    result = run_bass_kernel_spmd(nc, [arrays], core_ids=[0])
    return result.results[0]["out"]
```

```python
from contextlib import ExitStack

import concourse.bass as bass
from concourse import mybir

ALU = mybir.AluOpType
ACT = mybir.ActivationFunctionType
AX = mybir.AxisListType
F32 = mybir.dt.float32
F32R = mybir.dt.float32r
F16 = mybir.dt.float16
I32 = mybir.dt.int32

P = 128
DH = 64
VE = DH + 1
LN_EPS = 1e-5
DEQUANT = 1.0 / 127.0
X_SCALE = 64.0
V_LOG = 9
V_SCALE = 2.0 ** V_LOG
W_SCALE = 256.0


def build(nc, X, WqT, WkT, WvT, WoT, bo, WgT, WuT, WdT, out):
    NB, N, D = X.shape
    HD = WqT.shape[1]
    FF = WgT.shape[1]
    C = N // P
    NP = HD // P
    NF = FF // P
    assert D == P and N == C * P and C == 4 and NP == 8 and NF == 3

    x_dram = X.rearrange("b (c p) d -> b p c d", p=P)
    out_dram = out.rearrange("b (c p) d -> b p c d", p=P)

    with ExitStack() as ctx:
        def sb(name, shape, dt=F32):
            return ctx.enter_context(nc.sbuf_tensor(name, shape, dt))

        def pb(name):
            return ctx.enter_context(nc.psum_tensor(name, [P, 512], F32))

        def sem(name):
            return ctx.enter_context(nc.semaphore(name))

        wq = sb("wq", [P, HD])
        wk = sb("wk", [P, HD])
        wv = sb("wv", [P, HD])
        wo = sb("wo", [P, NP, D])
        bo_col = sb("bo_col", [P, 1])
        wg_i = sb("wg_i", [P, FF], I32)
        wu_i = sb("wu_i", [P, FF], I32)
        wd_i = sb("wd_i", [P, NF, D], I32)
        wg = sb("wg", [P, FF])
        wu = sb("wu", [P, FF])
        wd = sb("wd", [P, NF, D])
        wv_s = sb("wv_s", [P, HD])
        wo_s = sb("wo_s", [P, NP, D])
        wq_p = [sb(f"wq_{x}", [P, HD], F32R) for x in ("hi", "lo")]
        wk_p = [sb(f"wk_{x}", [P, HD], F32R) for x in ("hi", "lo")]
        wv_p = [sb(f"wv_{x}", [P, HD], F16) for x in ("hi", "lo")]
        wo_p = [sb(f"wo_{x}", [P, NP, D], F32R) for x in ("hi", "lo")]
        wg_p = [sb(f"wg_{x}", [P, FF], F32R) for x in ("hi", "lo")]
        wu_p = [sb(f"wu_{x}", [P, FF], F32R) for x in ("hi", "lo")]
        wd_p = [sb(f"wd_{x}", [P, NF, D], F32R) for x in ("hi", "lo")]
        wv_sq = sb("wv_sq", [P, HD])
        row_sq = sb("row_sq", [P, NP])
        exp_sq = sb("exp_sq", [P, NP], I32)
        exp_biased = sb("exp_biased", [P, NP], I32)
        exp_half = sb("exp_half", [P, NP], I32)
        exp_down = sb("exp_down", [P, NP], I32)
        exp_up = sb("exp_up", [P, NP], I32)
        scale_down = sb("scale_down", [P, NP], I32)
        scale_up = sb("scale_up", [P, NP], I32)
        down_diag = sb("down_diag", [P, NP, P], F32R)
        ones_r = sb("ones_r", [P, P], F32R)
        ident = sb("ident", [P, P])
        ones = sb("ones", [P, P])
        w_ones = sb("w_ones", [P, P], F16)
        causal = sb("causal", [P, P])
        head_sum = sb("head_sum", [P, 32])
        norm_pick = sb("norm_pick", [P, 4])
        head_rows = sb("head_rows", [P, P])
        minus_half = sb("minus_half", [P, C])
        x_in = sb("x_in", [P, C, D])
        x_res = sb("x_res", [P, C, D])
        ln_stats = sb("ln_stats", [P, C, 6])
        ln_sum = sb("ln_sum", [P, C])
        ln_gap = sb("ln_gap", [P, C])
        ln_dev = sb("ln_dev", [P, C])
        ln_gap2 = sb("ln_gap2", [P, C])
        ln_dev2 = sb("ln_dev2", [P, C])
        ln_mean = sb("ln_mean", [P, C])
        ln_var = sb("ln_var", [P, C])
        ln_rstd = sb("ln_rstd", [P, C])
        xn = sb("xn", [P, C, D])
        xr_hi = sb("xr_hi", [P, N], F32R)
        xr_lo = sb("xr_lo", [P, N], F32R)
        xh_hi = sb("xh_hi", [P, N], F16)
        xh_lo = sb("xh_lo", [P, N], F16)
        silu_gate = sb("silu_gate", [P, N])
        hidden = sb("hidden", [P, N])
        hid_hi = sb("hid_hi", [P, NF, N], F32R)
        hid_lo = sb("hid_lo", [P, NF, N], F32R)
        gate = sb("gate", [P, N])
        mixed = sb("mixed", [P, N])
        out_sb = sb("out_sb", [P, C, D])
        qT = sb("qT", [P, N])
        q_norm = sb("q_norm", [P, N])
        kT = sb("kT", [P, N])
        v1 = sb("v1", [P, C, 2, VE])
        v_hi = sb("v_hi", [P, 2, C, 2, VE], F16)
        v_lo = sb("v_lo", [P, 2, C, 2, VE], F16)
        v_sum = sb("v_sum", [P, 2, 2, VE])
        sum_hi = sb("sum_hi", [P, 2, 2, VE], F16)
        sum_lo = sb("sum_lo", [P, 2, 2, VE], F16)
        q_sq = sb("q_sq", [P, N])
        k_sq = sb("k_sq", [P, N])
        k_tok = sb("k_tok", [P, 3, P])
        state = sb("state", [P, 3, 2, VE])
        weights = sb("weights", [P, 2, C, P])
        w_hi = sb("w_hi", [P, 2, C, P], F16)
        w_lo = sb("w_lo", [P, 2, C, P], F16)
        norm_max = sb("norm_max", [P, 1])
        norm_cols = sb("norm_cols", [P, 4])
        norm_sq = sb("norm_sq", [P, 2])
        norm_inv = sb("norm_inv", [P, 2])
        rden = sb("rden", [P, C, 2, 1])
        o = sb("o", [P, C, 2, DH])
        oT_hi = sb("oT_hi", [P, N], F32R)
        oT_lo = sb("oT_lo", [P, N], F32R)

        b_s = [pb("b_s0"), pb("b_s1")]
        b_q = pb("b_q")
        b_k = pb("b_k")
        b_v = pb("b_v")
        b_oT = pb("b_oT")
        b_x = pb("b_x")
        b_y = pb("b_y")

        def o_bank(i):
            return b_s[i][:, 0:4 * VE].rearrange("p (c h e) -> p c h e", c=2, h=2)

        st_ps = b_v[:, 0:3 * VE].rearrange("p (c e) -> p c e", c=3)
        nb_ps = b_q[:, 0:4]

        wv_in = sem("wv_in")
        wq_in = sem("wq_in")
        wk_in = sem("wk_in")
        ffn_in = sem("ffn_in")
        wo_in = sem("wo_in")
        x_loaded = sem("x_loaded")
        out_stored = sem("out_stored")
        scale_step = sem("scale_step")
        row_sq_ps = sem("row_sq_ps")
        wv_sq_ready = sem("wv_sq_ready")
        ones_r_ready = sem("ones_r_ready")
        diag_ready = sem("diag_ready")
        down_ps = sem("down_ps")
        wv_scaled = sem("wv_scaled")
        ffn_scaled = sem("ffn_scaled")
        wo_scaled = sem("wo_scaled")
        wq_hi_ready = sem("wq_hi_ready")
        wq_lo_ready = sem("wq_lo_ready")
        wk_hi_ready = sem("wk_hi_ready")
        wk_lo_ready = sem("wk_lo_ready")
        wv_hi_ready = sem("wv_hi_ready")
        wv_lo_ready = sem("wv_lo_ready")
        ffn_hi_ready = sem("ffn_hi_ready")
        ffn_lo_ready = sem("ffn_lo_ready")
        wo_hi_ready = sem("wo_hi_ready")
        wo_lo_ready = sem("wo_lo_ready")
        v_pad_ready = sem("v_pad_ready")
        fill_ready = sem("fill_ready")
        pool_const = sem("pool_const")
        zero_fill = sem("zero_fill")
        stats_done = sem("stats_done")
        moment_step = sem("moment_step")
        mean_ready = sem("mean_ready")
        var_ready = sem("var_ready")
        rstd_ready = sem("rstd_ready")
        xn_ready = sem("xn_ready")
        xnT_ps = sem("xnT_ps")
        xr_hi_ready = sem("xr_hi_ready")
        xh_hi_ready = sem("xh_hi_ready")
        xr_lo_ready = sem("xr_lo_ready")
        xh_lo_ready = sem("xh_lo_ready")
        x_res_ready = sem("x_res_ready")
        q_ps = sem("q_ps")
        q_ready = sem("q_ready")
        q_sq_ready = sem("q_sq_ready")
        k_ps = sem("k_ps")
        k_ready = sem("k_ready")
        k_sq_ready = sem("k_sq_ready")
        v_ps = sem("v_ps")
        v_hi_ready = sem("v_hi_ready")
        v_lo_ready = sem("v_lo_ready")
        v1_ready = sem("v1_ready")
        v_sum_a = sem("v_sum_a")
        v_sum_ready = sem("v_sum_ready")
        sum_hi_ready = sem("sum_hi_ready")
        sum_lo_ready = sem("sum_lo_ready")
        norms_ps = sem("norms_ps")
        norm_max_ready = sem("norm_max_ready")
        norm_cols_ready = sem("norm_cols_ready")
        nb_ready = sem("nb_ready")
        norm_sq_ready = sem("norm_sq_ready")
        norm_inv_ready = sem("norm_inv_ready")
        q_norm_ready = sem("q_norm_ready")
        k_tok_ps = sem("k_tok_ps")
        k_tok_ready = sem("k_tok_ready")
        state_ps = sem("state_ps")
        state_part = sem("state_part")
        scores_ps = sem("scores_ps")
        weights_ready = sem("weights_ready")
        w16_hi0_ready = sem("w16_hi0_ready")
        w16_hi1_ready = sem("w16_hi1_ready")
        w16_lo0_ready = sem("w16_lo0_ready")
        w16_lo1_ready = sem("w16_lo1_ready")
        o_ps = sem("o_ps")
        rden_ready = sem("rden_ready")
        o_ready = sem("o_ready")
        oT_ps = sem("oT_ps")
        oT_hi_ready = sem("oT_hi_ready")
        oT_lo_ready = sem("oT_lo_ready")
        y_part = sem("y_part")
        mixed_ready = sem("mixed_ready")
        gate_h_ps = sem("gate_h_ps")
        silu_h_ready = sem("silu_h_ready")
        up_ps = sem("up_ps")
        hidden_ready = sem("hidden_ready")
        hid_hi_ready = sem("hid_hi_ready")
        hid_lo_ready = sem("hid_lo_ready")
        ffn_ps = sem("ffn_ps")
        gate_ready = sem("gate_ready")
        final_ps = sem("final_ps")
        out_ready = sem("out_ready")

        halves = [slice(i * 4 * P, (i + 1) * 4 * P) for i in range(2)]

        def some(count):
            return not isinstance(count, int) or count > 0

        def batches(eng, body):
            body(0, True, False)
            with eng.Fori(1, NB - 1) as b:
                body(b, False, False)
            body(NB - 1, False, True)

        block = ctx.enter_context(nc.Block())

        @block.sync
        def _(sp):
            def load_x(b):
                sp.dma_start(x_in[:, :, :], x_dram[b]).then_inc(x_loaded, 16)

            def store(b):
                sp.wait_ge(out_ready, b + 1)
                sp.dma_start(out_dram[b], out_sb[:, :, :]).then_inc(out_stored, 16)

            load_x(0)
            sp.dma_start(wv[:, :], WvT).then_inc(wv_in, 16)
            sp.dma_start(wq[:, :], WqT).then_inc(wq_in, 16)
            sp.dma_start(wk[:, :], WkT).then_inc(wk_in, 16)
            sp.dma_start(wg_i[:, :], WgT).then_inc(ffn_in, 16)
            sp.dma_start(wu_i[:, :], WuT).then_inc(ffn_in, 16)
            sp.dma_start(wd_i[:, :, :], WdT.rearrange("(t p) d -> p t d", p=P)).then_inc(ffn_in, 16)
            sp.dma_start(wo[:, :, :], WoT.rearrange("(t p) d -> p t d", p=P)).then_inc(wo_in, 16)
            sp.dma_start(bo_col[:, :], bo.rearrange("(p o) -> p o", o=1)).then_inc(wo_in, 16)

            def body(b, first, last):
                if not first:
                    store(b - 1)
                if not last:
                    sp.wait_ge(x_res_ready, b + 1)
                    sp.wait_ge(xn_ready, b + 1)
                    load_x(b + 1)

            batches(sp, body)
            store(NB - 1)
            sp.wait_ge(out_stored, 16 * NB)

        @block.gpsimd
        def _(pool):
            pool.memset(minus_half[:, :], -0.5).then_inc(fill_ready, 1)
            pool.memset(ones[:, :], 1.0).then_inc(fill_ready, 1)
            pool.memset(ident[:, :], 0.0).then_inc(zero_fill, 1)
            pool.memset(causal[:, :], 1.0).then_inc(zero_fill, 1)
            pool.memset(head_sum[:, :], 0.0).then_inc(zero_fill, 1)
            pool.memset(norm_pick[:, :], 0.0).then_inc(zero_fill, 1)
            pool.memset(head_rows[:, :], 0.0).then_inc(zero_fill, 1)
            pool.wait_ge(zero_fill, 5)
            pool.affine_select(out=ident[:, :], in_=ident[:, :], compare_op=ALU.not_equal, fill=1.0, base=0,
                               pattern=[[-1, P]], channel_multiplier=1).then_inc(pool_const, 1)
            pool.affine_select(out=causal[:, :], in_=causal[:, :], compare_op=ALU.is_ge, fill=0.0, base=0,
                               pattern=[[1, P]], channel_multiplier=-1).then_inc(pool_const, 1)
            for h in range(2):
                pool.wait_ge(pool_const, 2 + h)
                pool.memset(head_sum[h * DH:(h + 1) * DH, h:h + 1], 1.0).then_inc(pool_const, 1)
            for g in range(4):
                quadrant = slice(32 * g, 32 * g + 32)
                pool.wait_ge(pool_const, 4 + 3 * g)
                pool.memset(norm_pick[quadrant, g:g + 1], W_SCALE ** -2 if g < 2 else 1.0).then_inc(pool_const, 1)
                for h in range(2):
                    cols = head_rows[quadrant, h * DH:(h + 1) * DH]
                    pool.affine_select(out=cols, in_=cols, compare_op=ALU.not_equal, fill=1.0, base=-h,
                                       pattern=[[0, DH]], channel_multiplier=1).then_inc(pool_const, 1)

            def ln_rstd_of(b):
                pool.wait_ge(var_ready, b + 1)
                pool.tensor_tensor(ln_rstd[:, :], ln_var[:, :], minus_half[:, :], ALU.pow).then_inc(rstd_ready, 1)

            def value_sums(n):
                pool.wait_ge(v1_ready, n + 1)
                if some(n):
                    pool.wait_ge(sum_hi_ready, n)
                    pool.wait_ge(sum_lo_ready, n)
                pool.tensor_tensor(v_sum[:, 0], v1[:, 0], v1[:, 1], ALU.add).then_inc(v_sum_a, 1)
                pool.wait_ge(v_sum_a, n + 1)
                pool.tensor_tensor(v_sum[:, 1], v_sum[:, 0], v1[:, 2], ALU.add).then_inc(v_sum_ready, 1)

            def value_sums_lo(n):
                pool.wait_ge(sum_hi_ready, n + 1)
                if some(n):
                    pool.wait_ge(o_ps, 2 * n)
                pool.tensor_tensor(sum_lo[:, :, :, :], v_sum[:, :, :, :], sum_hi[:, :, :, :], ALU.subtract)\
                    .then_inc(sum_lo_ready, 1)

            def weights_lo0(u):
                pool.wait_ge(w16_hi0_ready, u + 1)
                if some(2 * u):
                    pool.wait_ge(o_ps, 2 * u)
                pool.tensor_tensor(w_lo[:, 0], weights[:, 0], w_hi[:, 0], ALU.subtract).then_inc(w16_lo0_ready, 1)

            def invert_norms(n):
                pool.wait_ge(norm_sq_ready, n + 1)
                if some(n):
                    pool.wait_ge(q_norm_ready, n)
                pool.tensor_tensor(norm_inv[:, :], norm_sq[:, :], minus_half[:, 0:2], ALU.pow)\
                    .then_inc(norm_inv_ready, 1)

            def values_lo(n, par):
                pool.wait_ge(v_hi_ready, n + 1)
                pool.wait_ge(v1_ready, n + 1)
                if some(2 * n - 2):
                    pool.wait_ge(o_ps, 2 * n - 2)
                pool.tensor_tensor(v_lo[:, par, :, :, 0:DH].rearrange("p c h e -> p (c h) e"),
                                   v1[:, :, :, 0:DH].rearrange("p c h e -> p (c h) e"),
                                   v_hi[:, par, :, :, 0:DH].rearrange("p c h e -> p (c h) e"),
                                   ALU.subtract).then_inc(v_lo_ready, 1)

            pool.wait_ge(pool_const, 16)
            pool.wait_ge(fill_ready, 2)
            ln_rstd_of(0)
            pool.memset(state[:, :, :, :], 0.0).then_inc(pool_const, 1)
            pool.memset(w_ones[:, :], W_SCALE).then_inc(pool_const, 1)
            pool.memset(v1[:, :, :, :], 1.0).then_inc(v_pad_ready, 1)
            pool.memset(v_hi[:, :, :, :, :], 1.0).then_inc(v_pad_ready, 1)
            pool.memset(v_lo[:, :, :, :, :], 0.0).then_inc(v_pad_ready, 1)
            for i, (lo, w, hi) in enumerate((
                    (wg_p[1][:, :], wg[:, :], wg_p[0][:, :]), (wu_p[1][:, :], wu[:, :], wu_p[0][:, :]),
                    (wd_p[1][:, :, :], wd[:, :, :], wd_p[0][:, :, :]))):
                pool.wait_ge(ffn_hi_ready, i + 1)
                pool.tensor_tensor(lo, w, hi.bitcast(F32), ALU.subtract).then_inc(ffn_lo_ready, 1)
            pool.wait_ge(pool_const, 18)
            pool.wait_ge(v_pad_ready, 3)
            invert_norms(0)
            value_sums(0)
            values_lo(0, 0)
            value_sums_lo(0)

            def body(b, first, last):
                for t in range(NP):
                    u = b * NP + t
                    weights_lo0(u)
                    if t == 5 and not last:
                        ln_rstd_of(b + 1)
                    if not (last and t == NP - 1):
                        invert_norms(u + 1)
                        value_sums(u + 1)
                        values_lo(u + 1, (t + 1) % 2)
                        value_sums_lo(u + 1)

            batches(pool, body)

        @block.tensor
        def _(pe):
            def split_product(out_ps, stationary, moving, start=True, stop=True):
                (s_hi, s_lo), (m_hi, m_lo) = stationary, moving
                pe.matmul(out_ps, s_hi, m_hi, start=start, stop=False, skip_group_check=True)
                pe.matmul(out_ps, s_hi, m_lo, start=False, stop=False, skip_group_check=True)
                return pe.matmul(out_ps, s_lo, m_hi, start=False, stop=stop, skip_group_check=True)

            def tile(parts, t):
                return [w[:, t * P:(t + 1) * P] for w in parts]

            xr = (xr_hi[:, :], xr_lo[:, :])

            def qk_weights(half):
                pe.wait_ge(wq_hi_ready, half)
                pe.wait_ge(wq_lo_ready, half)
                pe.wait_ge(wk_hi_ready, half)
                pe.wait_ge(wk_lo_ready, half)

            def v_weights(half):
                pe.wait_ge(wv_hi_ready, half)
                pe.wait_ge(wv_lo_ready, half)

            def ffn_weights(count):
                pe.wait_ge(ffn_hi_ready, count)
                pe.wait_ge(ffn_lo_ready, count)

            def project_qk(n, t):
                if some(n):
                    pe.wait_ge(norm_sq_ready, n)
                    pe.wait_ge(q_ready, n)
                split_product(b_q[:, :], tile(wq_p, t), xr).then_inc(q_ps, 1)
                if some(n):
                    pe.wait_ge(k_tok_ready, n)
                split_product(b_k[:, :], tile(wk_p, t), xr).then_inc(k_ps, 1)

            def project_v(n, t):
                if some(6 * n):
                    pe.wait_ge(state_part, 6 * n)
                for c in range(C):
                    mm = split_product(b_v[:, c * P:(c + 1) * P], tile((xh_hi, xh_lo), c), tile(wv_p, t))
                mm.then_inc(v_ps, 1)

            def norms(n):
                pe.wait_ge(q_ready, n + 1)
                pe.wait_ge(q_sq_ready, n + 1)
                for g in range(2):
                    pe.matmul(b_q[32 * g:32 * g + 32, 0:N // 2], head_sum[:, :],
                              q_sq[:, g * (N // 2):(g + 1) * (N // 2)], start=True, stop=True)
                pe.wait_ge(k_sq_ready, n + 1)
                for g in range(2, 4):
                    mm = pe.matmul(b_q[32 * g:32 * g + 32, 0:N // 2], head_sum[:, :],
                                   k_sq[:, (g - 2) * (N // 2):(g - 1) * (N // 2)], start=True, stop=True)
                mm.then_inc(norms_ps, 1)

            def keys_by_token(n):
                pe.wait_ge(k_ready, n + 1)
                pe.wait_ge(k_sq_ready, n + 1)
                for c in range(3):
                    mm = pe.transpose(b_k[:, c * P:(c + 1) * P], kT[:, c * P:(c + 1) * P], ident[:, :])
                mm.then_inc(k_tok_ps, 1)

            def states(n):
                pe.wait_ge(k_tok_ready, n + 1)
                pe.wait_ge(v1_ready, n + 1)
                for c in range(3):
                    for h in range(2):
                        mm = pe.matmul(st_ps[h * DH:(h + 1) * DH, c], k_tok[:, c, h * DH:(h + 1) * DH],
                                       v1[:, c, h, :], start=True, stop=True)
                mm.then_inc(state_ps, 1)

            def spread_norms(n):
                pe.wait_ge(norm_cols_ready, n + 1)
                pe.matmul(nb_ps, head_rows[:, :], norm_cols[:, :], start=True, stop=True).then_inc(nb_ready, 1)

            def scores(u):
                pe.wait_ge(q_norm_ready, u + 1)
                pe.wait_ge(k_ready, u + 1)
                for h in range(2):
                    if some(2 * u):
                        pe.wait_ge(o_ready, 2 * u - 1 + h)
                    for c in range(C):
                        rows = slice(h * DH, (h + 1) * DH)
                        mm = pe.matmul(b_s[h][:, c * P:(c + 1) * P], kT[rows, c * P:(c + 1) * P],
                                       q_norm[rows, c * P:(c + 1) * P], start=True, stop=True)
                    mm.then_inc(scores_ps, 1)

            def attend_sums(u, par):
                pe.wait_ge(weights_ready, 2 * u + 2)
                pe.wait_ge(v_hi_ready, u + 1)
                pe.wait_ge(v_lo_ready, u + 1)
                pe.wait_ge(sum_lo_ready, u + 1)
                pe.matmul(o_bank(0)[:, 1], w_ones[:, :], v_hi[:, par, 0], start=True, stop=False,
                          skip_group_check=True)
                pe.matmul(o_bank(0)[:, 1], w_ones[:, :], v_lo[:, par, 0], start=False, stop=False,
                          skip_group_check=True)
                pe.matmul(o_bank(1), w_ones[:, :], sum_hi[:, :, :, :], start=True, stop=False,
                          skip_group_check=True)
                pe.matmul(o_bank(1), w_ones[:, :], sum_lo[:, :, :, :], start=False, stop=False,
                          skip_group_check=True)

            def attend_states(u):
                pe.wait_ge(state_part, 6 * (u + 1))
                for c in range(1, C):
                    pe.matmul(o_bank(c // 2)[:, c % 2], q_norm[:, c * P:(c + 1) * P], state[:, c - 1],
                              start=False, stop=False, skip_group_check=True)

            def attend_own(u, par):
                pe.wait_ge(w16_lo0_ready, u + 1)
                pe.wait_ge(w16_lo1_ready, u + 1)
                for i in range(2):
                    for c in range(2 * i, 2 * i + 2):
                        for h in range(2):
                            mm = split_product(o_bank(i)[:, c % 2, h], (w_hi[:, h, c], w_lo[:, h, c]),
                                               (v_hi[:, par, c, h, :], v_lo[:, par, c, h, :]), start=False)
                    mm.then_inc(o_ps, 1)

            def turn_outputs(u):
                pe.wait_ge(o_ready, 2 * (u + 1))
                if some(u):
                    pe.wait_ge(oT_lo_ready, u)
                for c in range(C):
                    mm = pe.transpose(b_oT[:, c * P:(c + 1) * P], o[:, c].rearrange("p h e -> p (h e)"), ident[:, :])
                mm.then_inc(oT_ps, 1)

            def project_out(u, t, mixed_before):
                pe.wait_ge(oT_hi_ready, u + 1)
                pe.wait_ge(oT_lo_ready, u + 1)
                if t == 0:
                    if some(mixed_before):
                        pe.wait_ge(mixed_ready, mixed_before)
                split_product(b_y[:, :], [w[:, t, :] for w in wo_p], (oT_hi[:, :], oT_lo[:, :]),
                              start=(t == 0), stop=(t == NP - 1)).then_inc(y_part, 1)

            def ffn_gate(b, f):
                if f == 0:
                    if some(b):
                        pe.wait_ge(gate_ready, b)
                else:
                    pe.wait_ge(hidden_ready, b * NF + f)
                split_product(b_x[:, :], tile(wg_p, f), xr).then_inc(gate_h_ps, 1)

            def ffn_up(b, f):
                pe.wait_ge(silu_h_ready, b * NF + f + 1)
                if f == 0 and some(b):
                    pe.wait_ge(out_ready, b)
                split_product(b_x[:, :], tile(wu_p, f), xr).then_inc(up_ps, 1)

            def ffn_down(b, last):
                if not last:
                    pe.wait_ge(xr_lo_ready, b + 2)
                    pe.wait_ge(xh_lo_ready, b + 2)
                for f in range(NF):
                    pe.wait_ge(hid_hi_ready, b * NF + f + 1)
                    pe.wait_ge(hid_lo_ready, b * NF + f + 1)
                    mm = split_product(b_x[:, :], [w[:, f, :] for w in wd_p], (hid_hi[:, f, :], hid_lo[:, f, :]),
                                       start=(f == 0), stop=(f == NF - 1))
                mm.then_inc(ffn_ps, 1)

            def turn_xn(b):
                pe.wait_ge(xn_ready, b + 1)
                if some(b * NF):
                    pe.wait_ge(hidden_ready, b * NF)
                for c in range(C):
                    mm = pe.transpose(b_x[:, c * P:(c + 1) * P], xn[:, c, :], ident[:, :])
                mm.then_inc(xnT_ps, 1)

            def turn_mixed(b, silu_count):
                pe.wait_ge(mixed_ready, b + 1)
                pe.wait_ge(silu_h_ready, silu_count)
                for c in range(C):
                    mm = pe.transpose(b_x[:, c * P:(c + 1) * P], mixed[:, c * P:(c + 1) * P], ident[:, :])
                mm.then_inc(final_ps, 1)

            pe.wait_ge(pool_const, 16)
            pe.wait_ge(fill_ready, 2)
            pe.wait_ge(wv_sq_ready, 1)
            for t in range(NP):
                mm = pe.matmul(b_y[:, t:t + 1], wv_sq[:, t * P:(t + 1) * P], ones[:, 0:1], start=True, stop=True)
            mm.then_inc(row_sq_ps, 1)
            turn_xn(0)
            pe.wait_ge(ones_r_ready, 1)
            for i in range(2):
                pe.wait_ge(diag_ready, i + 1)
                pe.matmul(b_s[i][:, :], ones_r[:, :], down_diag[:, 4 * i:4 * i + 4, :], start=True, stop=True)\
                    .then_inc(down_ps, 1)
            pe.wait_ge(xr_hi_ready, 1)
            pe.wait_ge(xr_lo_ready, 1)
            qk_weights(1)
            project_qk(0, 0)
            pe.wait_ge(xh_hi_ready, 1)
            pe.wait_ge(xh_lo_ready, 1)
            v_weights(1)
            project_v(0, 0)
            pe.wait_ge(pool_const, 18)
            norms(0)
            keys_by_token(0)
            spread_norms(0)
            states(0)

            def body(b, first, last):
                for t in range(NP):
                    u = b * NP + t
                    par = t % 2
                    nt = (t + 1) % NP
                    more = not (last and t == NP - 1)
                    scores(u)
                    if more:
                        if t == NP - 1:
                            pe.wait_ge(xr_hi_ready, b + 2)
                            pe.wait_ge(xr_lo_ready, b + 2)
                        if first and t == 3:
                            qk_weights(2)
                        project_qk(u + 1, nt)
                        if first and t == 3:
                            v_weights(2)
                        if t == NP - 1:
                            pe.wait_ge(xh_hi_ready, b + 2)
                            pe.wait_ge(xh_lo_ready, b + 2)
                        project_v(u + 1, nt)
                    if not (first and t == 0):
                        turn_outputs(u - 1)
                    if t == 1 and not first:
                        turn_mixed(b - 1, b * NF + 1)
                    attend_sums(u, par)
                    if more:
                        norms(u + 1)
                        keys_by_token(u + 1)
                    attend_states(u)
                    if more:
                        spread_norms(u + 1)
                    if t == 6 and not last:
                        turn_xn(b + 1)
                    attend_own(u, par)
                    if more:
                        states(u + 1)
                    if first and t == 1:
                        pe.wait_ge(wo_hi_ready, 1)
                        pe.wait_ge(wo_lo_ready, 1)
                    if not (first and t == 0):
                        project_out(u - 1, (t - 1) % NP, b)
                    if first and t in (0, 1, 7):
                        ffn_weights(min(t, 2) + 1)
                    if t in (0, 2, 4):
                        ffn_gate(b, t // 2)
                    if t in (1, 3, 5):
                        ffn_up(b, t // 2)
                    if t == 7:
                        ffn_down(b, last)

            batches(pe, body)
            turn_outputs(NB * NP - 1)
            project_out(NB * NP - 1, NP - 1, NB - 1)
            pe.wait_ge(gate_ready, NB)
            turn_mixed(NB - 1, NB * NF)

        @block.scalar
        def _(act):
            def split_hi(out, value, ready, scale=1.0):
                act.activation(out, value, ACT.Copy, scale=scale).then_inc(ready, 1)

            def copy_qk(n, square_k_too=False):
                act.wait_ge(q_ps, n + 1)
                if some(n):
                    act.wait_ge(scores_ps, 2 * n)
                act.activation(qT[:, :], b_q[:, :], ACT.Copy).then_inc(q_ready, 1)
                act.wait_ge(k_ps, n + 1)
                if some(n):
                    act.wait_ge(norms_ps, n)
                act.activation(kT[:, :], b_k[:, :], ACT.Copy).then_inc(k_ready, 1)
                act.activation(q_sq[:, :], b_q[:, :], ACT.Square).then_inc(q_sq_ready, 1)
                if square_k_too:
                    act.activation(k_sq[:, :], b_k[:, :], ACT.Square).then_inc(k_sq_ready, 1)

            def copy_v(n, par):
                act.wait_ge(v_ps, n + 1)
                act.activation(v_hi[:, par, :, :, 0:DH].rearrange("p c h e -> p (c h) e"),
                               b_v[:, :].rearrange("p (c e) -> p c e", e=DH), ACT.Copy, scale=1.0 / X_SCALE)\
                    .then_inc(v_hi_ready, 1)
                if some(n):
                    act.wait_ge(state_ps, n)
                    act.wait_ge(v_sum_ready, n)
                    act.wait_ge(v_lo_ready, n)
                act.activation(v1[:, :, :, 0:DH].rearrange("p c h e -> p (c h) e"),
                               b_v[:, :].rearrange("p (c e) -> p c e", e=DH), ACT.Copy, scale=1.0 / X_SCALE)\
                    .then_inc(v1_ready, 1)

            def copy_k_tok(n):
                act.wait_ge(k_tok_ps, n + 1)
                act.activation(k_tok[:, :, :].rearrange("p c f -> p (c f)"), b_k[:, 0:3 * P], ACT.Copy)\
                    .then_inc(k_tok_ready, 1)

            def value_sums_hi(n):
                act.wait_ge(v_sum_ready, n + 1)
                if some(2 * n):
                    act.wait_ge(o_ps, 2 * n)
                act.activation(sum_hi[:, :, :, :], v_sum[:, :, :, :], ACT.Copy).then_inc(sum_hi_ready, 1)

            def weights_hi0(u):
                if some(2 * u):
                    act.wait_ge(o_ps, 2 * u)
                act.wait_ge(weights_ready, 2 * u + 1)
                act.activation(w_hi[:, 0], weights[:, 0], ACT.Copy).then_inc(w16_hi0_ready, 1)

            def copy_oT(u):
                act.wait_ge(oT_ps, u + 1)
                if some(u):
                    act.wait_ge(y_part, u)
                act.activation(oT_hi[:, :], b_oT[:, :], ACT.Copy).then_inc(oT_hi_ready, 1)

            def copy_xnT(b):
                act.wait_ge(xnT_ps, b + 1)
                if some(b * NP):
                    act.wait_ge(v_ps, b * NP)
                if some(b * NF):
                    act.wait_ge(up_ps, b * NF)
                act.activation(xr_hi[:, :], b_x[:, :], ACT.Copy).then_inc(xr_hi_ready, 1)
                act.activation(xh_hi[:, :], b_x[:, :], ACT.Copy, scale=X_SCALE).then_inc(xh_hi_ready, 1)

            def silu_hidden(b, f):
                act.wait_ge(gate_h_ps, b * NF + f + 1)
                if some(b * NF + f):
                    act.wait_ge(hidden_ready, b * NF + f)
                act.activation(silu_gate[:, :], b_x[:, :], ACT.Silu).then_inc(silu_h_ready, 1)

            def hidden_hi(b, f):
                act.wait_ge(hidden_ready, b * NF + f + 1)
                if some(b):
                    act.wait_ge(ffn_ps, b)
                act.activation(hid_hi[:, f, :], hidden[:, :], ACT.Copy).then_inc(hid_hi_ready, 1)

            act.wait_ge(wv_in, 16)
            act.activation(wv_sq[:, :], wv[:, :], ACT.Square).then_inc(wv_sq_ready, 1)
            act.wait_ge(wq_in, 16)
            act.activation(wq_p[0][:, halves[0]], wq[:, halves[0]], ACT.Copy).then_inc(wq_hi_ready, 1)
            act.wait_ge(wk_in, 16)
            act.activation(wk_p[0][:, halves[0]], wk[:, halves[0]], ACT.Copy).then_inc(wk_hi_ready, 1)
            copy_xnT(0)
            act.activation(wq_p[0][:, halves[1]], wq[:, halves[1]], ACT.Copy).then_inc(wq_hi_ready, 1)
            act.activation(wk_p[0][:, halves[1]], wk[:, halves[1]], ACT.Copy).then_inc(wk_hi_ready, 1)
            for i in range(2):
                act.wait_ge(wv_scaled, i + 1)
                act.activation(wv_p[0][:, halves[i]], wv_s[:, halves[i]], ACT.Copy).then_inc(wv_hi_ready, 1)
            for i, (part, w) in enumerate(((wg_p[0][:, :], wg[:, :]), (wu_p[0][:, :], wu[:, :]),
                                           (wd_p[0][:, :, :], wd[:, :, :]))):
                act.wait_ge(ffn_scaled, i + 1)
                act.activation(part, w, ACT.Copy).then_inc(ffn_hi_ready, 1)
            act.wait_ge(v_pad_ready, 3)
            copy_qk(0)
            copy_v(0, 0)
            copy_k_tok(0)
            value_sums_hi(0)
            act.wait_ge(wo_scaled, 1)
            act.activation(wo_p[0][:, :, :], wo_s[:, :, :], ACT.Copy).then_inc(wo_hi_ready, 1)

            def body(b, first, last):
                for t in range(NP):
                    u = b * NP + t
                    more = not (last and t == NP - 1)
                    weights_hi0(u)
                    if more:
                        copy_qk(u + 1, t == 7)
                    if not (first and t == 0):
                        copy_oT(u - 1)
                    if more:
                        copy_v(u + 1, (t + 1) % 2)
                        copy_k_tok(u + 1)
                    if t == 6 and not last:
                        copy_xnT(b + 1)
                    if t in (2, 4, 6):
                        hidden_hi(b, t // 2 - 1)
                    if more:
                        value_sums_hi(u + 1)
                    if t in (0, 2, 4):
                        silu_hidden(b, t // 2)
                    if t == 7:
                        act.wait_ge(ffn_ps, b + 1)
                        if some(b):
                            act.wait_ge(mixed_ready, b)
                        act.activation(gate[:, :], b_x[:, :], ACT.Silu).then_inc(gate_ready, 1)

            batches(act, body)
            copy_oT(NB * NP - 1)

        @block.vector
        def _(dve):
            def ln_statistics(b):
                dve.wait_ge(x_loaded, 16 * (b + 1))
                for c in range(C):
                    dve.bn_stats(ln_stats[:, c, :], x_in[:, c, :]).then_inc(stats_done, 1)

            def ln_moments(b):
                dve.wait_ge(stats_done, (b + 1) * C)
                dve.tensor_tensor(ln_gap[:, :], ln_stats[:, :, 1], ln_stats[:, :, 4], ALU.subtract)\
                    .then_inc(moment_step, 1)
                dve.tensor_tensor(ln_sum[:, :], ln_stats[:, :, 1], ln_stats[:, :, 4], ALU.add)\
                    .then_inc(moment_step, 1)
                dve.tensor_tensor(ln_dev[:, :], ln_stats[:, :, 2], ln_stats[:, :, 5], ALU.add)\
                    .then_inc(moment_step, 1)
                dve.wait_ge(moment_step, 5 * b + 3)
                dve.scalar_tensor_tensor(out=ln_gap2[:, :], in0=ln_gap[:, :], scalar=0.25, in1=ln_gap[:, :],
                                         op0=ALU.mult, op1=ALU.mult).then_inc(moment_step, 1)
                dve.tensor_scalar(ln_dev2[:, :], ln_dev[:, :], 1.0 / D, LN_EPS, ALU.mult, ALU.add)\
                    .then_inc(moment_step, 1)
                dve.tensor_scalar(ln_mean[:, :], ln_sum[:, :], 0.5, None, ALU.mult).then_inc(mean_ready, 1)
                dve.wait_ge(moment_step, 5 * b + 5)
                dve.tensor_tensor(ln_var[:, :], ln_dev2[:, :], ln_gap2[:, :], ALU.add).then_inc(var_ready, 1)

            def ln_apply(b):
                dve.wait_ge(rstd_ready, b + 1)
                dve.wait_ge(mean_ready, b + 1)
                if some(b):
                    dve.wait_ge(xnT_ps, b)
                for c in range(C):
                    last = dve.tensor_scalar(xn[:, c, :], x_in[:, c, :], ln_mean[:, c:c + 1], ln_rstd[:, c:c + 1],
                                             ALU.subtract, ALU.mult)
                last.then_inc(xn_ready, 1)

            def split_xr(b):
                dve.wait_ge(xr_hi_ready, b + 1)
                dve.wait_ge(xh_hi_ready, b + 1)
                dve.tensor_tensor(xr_lo[:, :], b_x[:, :], xr_hi[:, :].bitcast(F32), ALU.subtract)\
                    .then_inc(xr_lo_ready, 1)

            def split_xh(b):
                dve.wait_ge(xh_hi_ready, b + 1)
                dve.scalar_tensor_tensor(out=xh_lo[:, :], in0=b_x[:, :], scalar=X_SCALE, in1=xh_hi[:, :],
                                         op0=ALU.mult, op1=ALU.subtract).then_inc(xh_lo_ready, 1)

            def normalise_q(n):
                dve.wait_ge(norm_inv_ready, n + 1)
                dve.wait_ge(q_ready, n + 1)
                if some(2 * n):
                    dve.wait_ge(o_ps, 2 * n)
                dve.tensor_scalar(q_norm[:, :], qT[:, :], norm_inv[:, 0:1], norm_inv[:, 1:2], ALU.mult, ALU.mult)\
                    .then_inc(q_norm_ready, 1)

            def make_weights(u, h):
                dve.wait_ge(scores_ps, 2 * u + h + 1)
                if h == 0 and some(u):
                    dve.wait_ge(w16_lo0_ready, u)
                dve.scalar_tensor_tensor(out=weights[:, h], in0=b_s[h][:, :].rearrange("p (c q) -> p c q", c=C),
                                         scalar=W_SCALE, in1=causal_all, op0=ALU.add, op1=ALU.mult)\
                    .then_inc(weights_ready, 1)

            causal_all = causal[:, :].rearrange("p (o q) -> p o q", o=1).to_broadcast([P, C, P])

            def split_weights1(u):
                dve.wait_ge(weights_ready, 2 * u + 2)
                if some(2 * u):
                    dve.wait_ge(o_ps, 2 * u)
                dve.tensor_copy(w_hi[:, 1], weights[:, 1]).then_inc(w16_hi1_ready, 1)
                dve.wait_ge(w16_hi1_ready, u + 1)
                dve.tensor_tensor(w_lo[:, 1], weights[:, 1], w_hi[:, 1], ALU.subtract).then_inc(w16_lo1_ready, 1)

            def outputs_lo(u):
                dve.wait_ge(oT_hi_ready, u + 1)
                dve.tensor_tensor(oT_lo[:, :], b_oT[:, :], oT_hi[:, :].bitcast(F32), ALU.subtract)\
                    .then_inc(oT_lo_ready, 1)

            def hidden_lo(b, f):
                dve.wait_ge(hid_hi_ready, b * NF + f + 1)
                dve.tensor_tensor(hid_lo[:, f, :], hidden[:, :], hid_hi[:, f, :].bitcast(F32), ALU.subtract)\
                    .then_inc(hid_lo_ready, 1)

            def normalise(u):
                for i in range(2):
                    dve.wait_ge(o_ps, 2 * u + i + 1)
                    dve.reciprocal(rden[:, 2 * i:2 * i + 2], o_bank(i)[:, :, :, DH:VE]).then_inc(rden_ready, 1)
                if some(u):
                    dve.wait_ge(oT_ps, u)
                for i in range(2):
                    dve.wait_ge(rden_ready, 2 * u + i + 1)
                    dve.tensor_tensor(o[:, 2 * i:2 * i + 2], o_bank(i)[:, :, :, 0:DH],
                                      rden[:, 2 * i:2 * i + 2].to_broadcast([P, 2, 2, DH]), ALU.mult)\
                        .then_inc(o_ready, 1)

            def reduce_norms(n):
                dve.wait_ge(norms_ps, n + 1)
                dve.tensor_reduce(norm_max[:, :], b_q[:, 0:N // 2], AX.X, ALU.max).then_inc(norm_max_ready, 1)
                dve.wait_ge(norm_max_ready, n + 1)
                if some(n):
                    dve.wait_ge(nb_ready, n)
                dve.tensor_scalar(norm_cols[:, :], norm_pick[:, :], norm_max[:, :], None, ALU.mult)\
                    .then_inc(norm_cols_ready, 1)

            def sum_states(n, c):
                if c == 0:
                    dve.wait_ge(state_ps, n + 1)
                else:
                    dve.wait_ge(state_part, 6 * n + 2 * c)
                for h in range(2):
                    rows = slice(h * DH, (h + 1) * DH)
                    if c == 0:
                        ins = dve.tensor_copy(state[rows, 0, h], st_ps[rows, 0])
                    else:
                        ins = dve.tensor_tensor(state[rows, c, h], st_ps[rows, c], state[rows, c - 1, h], ALU.add)
                    ins.then_inc(state_part, 1)

            def copy_norms(n):
                dve.wait_ge(nb_ready, n + 1)
                if some(n):
                    dve.wait_ge(norm_inv_ready, n)
                dve.tensor_reduce(norm_sq[:, :], nb_ps.rearrange("p (j s) -> p j s", s=2), AX.X, ALU.max)\
                    .then_inc(norm_sq_ready, 1)

            def mix(b):
                dve.wait_ge(y_part, (b + 1) * NP)
                dve.wait_ge(gate_ready, b + 1)
                if some(b):
                    dve.wait_ge(final_ps, b)
                dve.scalar_tensor_tensor(out=mixed[:, :], in0=b_y[:, :], scalar=bo_col[:, :], in1=gate[:, :],
                                         op0=ALU.add, op1=ALU.mult).then_inc(mixed_ready, 1)

            def add_residual(b):
                dve.wait_ge(final_ps, b + 1)
                dve.wait_ge(x_res_ready, b + 1)
                if some(16 * b):
                    dve.wait_ge(out_stored, 16 * b)
                dve.tensor_tensor(out_sb[:, :, :].rearrange("p c d -> p (c d)"), b_x[:, :],
                                  x_res[:, :, :].rearrange("p c d -> p (c d)"), ALU.add).then_inc(out_ready, 1)

            def keep_x(b):
                if some(b):
                    dve.wait_ge(out_ready, b)
                dve.tensor_copy(x_res[:, :, :], x_in[:, :, :]).then_inc(x_res_ready, 1)

            def square_k(n):
                dve.wait_ge(k_ready, n + 1)
                if some(n):
                    dve.wait_ge(norms_ps, n)
                dve.tensor_tensor(k_sq[:, :], kT[:, :], kT[:, :], ALU.mult).then_inc(k_sq_ready, 1)

            def multiply_up(b, f):
                dve.wait_ge(up_ps, b * NF + f + 1)
                dve.tensor_tensor(hidden[:, :], b_x[:, :], silu_gate[:, :], ALU.mult)\
                    .then_inc(hidden_ready, 1)

            def qk_lo(i):
                cols = halves[i]
                dve.wait_ge(wq_hi_ready, i + 1)
                dve.tensor_tensor(wq_p[1][:, cols], wq[:, cols], wq_p[0][:, cols].bitcast(F32), ALU.subtract)\
                    .then_inc(wq_lo_ready, 1)
                dve.wait_ge(wk_hi_ready, i + 1)
                dve.tensor_tensor(wk_p[1][:, cols], wk[:, cols], wk_p[0][:, cols].bitcast(F32), ALU.subtract)\
                    .then_inc(wk_lo_ready, 1)

            def scale_wv(i):
                dve.wait_ge(down_ps, i + 1)
                dve.tensor_tensor(wv_s[:, halves[i]], wv[:, halves[i]], b_s[i][:, :], ALU.mult)\
                    .then_inc(wv_scaled, 1)

            def v_lo_part(i):
                cols = halves[i]
                dve.wait_ge(wv_hi_ready, i + 1)
                dve.tensor_tensor(wv_p[1][:, cols], wv_s[:, cols], wv_p[0][:, cols], ALU.subtract)\
                    .then_inc(wv_lo_ready, 1)

            ln_statistics(0)
            ln_moments(0)
            dve.wait_ge(fill_ready, 2)
            dve.tensor_copy(ones_r[:, :], ones[:, :]).then_inc(ones_r_ready, 1)
            ln_apply(0)
            qk_lo(0)
            dve.wait_ge(row_sq_ps, 1)
            dve.tensor_copy(row_sq[:, :], b_y[:, 0:NP]).then_inc(scale_step, 1)
            dve.wait_ge(scale_step, 1)
            dve.tensor_scalar(exp_sq[:, :], row_sq[:, :].bitcast(I32), 23, None, ALU.logical_shift_right)\
                .then_inc(scale_step, 1)
            dve.wait_ge(scale_step, 2)
            dve.tensor_scalar(exp_biased[:, :], exp_sq[:, :], 127.0, None, ALU.add).then_inc(scale_step, 1)
            dve.wait_ge(scale_step, 3)
            dve.tensor_scalar(exp_half[:, :], exp_biased[:, :], 1, None, ALU.logical_shift_right)\
                .then_inc(scale_step, 1)
            dve.wait_ge(scale_step, 4)
            dve.tensor_scalar(exp_down[:, :], exp_half[:, :], -1.0, 254.0 + V_LOG, ALU.mult, ALU.add)\
                .then_inc(scale_step, 1)
            dve.tensor_scalar(exp_up[:, :], exp_half[:, :], -1.0 * V_LOG, None, ALU.add).then_inc(scale_step, 1)
            dve.wait_ge(scale_step, 6)
            dve.tensor_scalar(scale_down[:, :], exp_down[:, :], 23, None, ALU.logical_shift_left)\
                .then_inc(scale_step, 1)
            dve.tensor_scalar(scale_up[:, :], exp_up[:, :], 23, None, ALU.logical_shift_left)\
                .then_inc(scale_step, 1)
            dve.wait_ge(scale_step, 8)
            dve.wait_ge(pool_const, 1)
            down_col = scale_down[:, :].bitcast(F32).rearrange("p (t o) -> p t o", o=1)
            up_col = scale_up[:, :].bitcast(F32).rearrange("p (t o) -> p t o", o=1)
            for i in range(2):
                dve.tensor_tensor(down_diag[:, 4 * i:4 * i + 4, :],
                                  ident[:, :].rearrange("p (o q) -> p o q", o=1).to_broadcast([P, 4, P]),
                                  down_col[:, 4 * i:4 * i + 4].to_broadcast([P, 4, P]), ALU.mult)\
                    .then_inc(diag_ready, 1)

            split_xr(0)
            scale_wv(0)
            split_xh(0)
            scale_wv(1)
            v_lo_part(0)
            dve.wait_ge(ffn_in, 48)
            for dst, src in ((wg[:, :], wg_i[:, :]), (wu[:, :], wu_i[:, :]), (wd[:, :, :], wd_i[:, :, :])):
                dve.tensor_scalar(dst, src, DEQUANT, None, ALU.mult).then_inc(ffn_scaled, 1)
            qk_lo(1)
            dve.wait_ge(pool_const, 18)
            dve.wait_ge(v_pad_ready, 3)
            square_k(0)
            reduce_norms(0)
            copy_norms(0)
            normalise_q(0)
            v_lo_part(1)
            dve.wait_ge(wo_in, 32)
            dve.tensor_tensor(wo_s[:, :, :], wo[:, :, :], up_col.to_broadcast([P, NP, D]), ALU.mult)\
                .then_inc(wo_scaled, 1)

            def body(b, first, last):
                for t in range(NP):
                    u = b * NP + t
                    more = not (last and t == NP - 1)
                    sum_states(u, 0)
                    make_weights(u, 0)
                    sum_states(u, 1)
                    if t == 7:
                        sum_states(u, 2)
                    make_weights(u, 1)
                    if t != 7:
                        sum_states(u, 2)
                    split_weights1(u)
                    if t != 7:
                        square_k(u + 1)
                    if t in (2, 4, 6):
                        multiply_up(b, t // 2 - 1)
                    if more:
                        reduce_norms(u + 1)
                    if not (first and t == 0):
                        outputs_lo(u - 1)
                    if more:
                        copy_norms(u + 1)
                    if t == 1 and not first:
                        add_residual(b - 1)
                    if t in (3, 5):
                        hidden_lo(b, t // 2 - 1)
                    if t == 2:
                        keep_x(b)
                    if t == 6:
                        normalise_q(u + 1)
                    normalise(u)
                    if more and t != 6:
                        normalise_q(u + 1)
                    if t == 7:
                        hidden_lo(b, NF - 1)
                    if t == 3 and not last:
                        ln_statistics(b + 1)
                    if t == 4 and not last:
                        ln_moments(b + 1)
                    if t == 5 and not last:
                        ln_apply(b + 1)
                    if t == 6 and not last:
                        split_xr(b + 1)
                        split_xh(b + 1)
                    if t == 0 and not first:
                        mix(b - 1)
                    if first and t == 0:
                        dve.wait_ge(wo_hi_ready, 1)
                        dve.tensor_tensor(wo_p[1][:, :, :], wo_s[:, :, :], wo_p[0][:, :, :].bitcast(F32),
                                          ALU.subtract).then_inc(wo_lo_ready, 1)

            batches(dve, body)
            outputs_lo(NB * NP - 1)
            mix(NB - 1)
            add_residual(NB - 1)


def kernel(L0_attn_X, L0_attn_Wq, L0_attn_Wk, L0_attn_Wv, L0_attn_Wo, L0_attn_bo,
           L0_ffn_w_gate, L0_ffn_w_up, L0_ffn_w_down):
    import numpy as np
    import concourse.bacc as bacc
    from concourse.bass_utils import run_bass_kernel_spmd

    arrays = {
        "X": np.ascontiguousarray(L0_attn_X),
        "WqT": np.ascontiguousarray(np.asarray(L0_attn_Wq).T),
        "WkT": np.ascontiguousarray(np.asarray(L0_attn_Wk).T),
        "WvT": np.ascontiguousarray(np.asarray(L0_attn_Wv).T),
        "WoT": np.ascontiguousarray(np.asarray(L0_attn_Wo).T),
        "bo": np.ascontiguousarray(L0_attn_bo),
        "WgT": np.ascontiguousarray(np.asarray(L0_ffn_w_gate).T),
        "WuT": np.ascontiguousarray(np.asarray(L0_ffn_w_up).T),
        "WdT": np.ascontiguousarray(np.asarray(L0_ffn_w_down).T),
    }
    nc = bacc.Bacc("TRN2", target_bir_lowering=False, num_devices=1)
    args = [nc.dram_tensor(n, v.shape, mybir.dt.from_np(v.dtype), kind="ExternalInput").ap()
            for n, v in arrays.items()]
    out = nc.dram_tensor("out", arrays["X"].shape, F32, kind="ExternalOutput").ap()
    build(nc, *args, out)
    result = run_bass_kernel_spmd(nc, [arrays], core_ids=[0])
    return result.results[0]["out"]
```
